# Optimizing a Trainium2 kernel written in Bass

```python
import numpy as np
import jax
import jax.numpy as jnp

def _softmax(x, axis=-1):
    return jax.nn.softmax(x, axis=axis)

def _gelu(x):
    return jax.nn.gelu(x, approximate=True)

def _silu(x):
    return jax.nn.silu(x)

def _sigmoid(x):
    return jax.nn.sigmoid(x)

def _layernorm(x, axis=-1, eps=1e-05):
    m = jnp.mean(x, axis=axis, keepdims=True)
    v = jnp.var(x, axis=axis, keepdims=True)
    return (x - m) / jnp.sqrt(v + eps)

def _scatter_add(tgt, idx, src, axis=0):
    return tgt.at[idx].add(src)

def _segment_sum(src, seg, n):
    return jax.ops.segment_sum(src, seg, n)
kernel_name = 'mk_cond_resid_d2_seqx_r2_395a33'

def setup_inputs(seed: int=0):
    np.random.seed(seed)
    _w = jnp.asarray

    def _rec_inputs():
        import jax
        import jax.numpy as jnp
        _rk = jax.random.key(seed)
        x = 0.5 + 0.2886 * jax.random.normal(jax.random.fold_in(_rk, 1), (2, 2048, 512), jnp.float32)
        _lenS = 2048 - jax.random.randint(jax.random.fold_in(_rk, 7), (2,), 0, max(1, 2048 // 4) + 1, jnp.int32)
        _lenS2 = 2048 - jax.random.randint(jax.random.fold_in(_rk, 8), (2,), 0, max(1, 2048 // 4) + 1, jnp.int32)
        fside_BxS_0 = jax.random.uniform(jax.random.fold_in(_rk, 11), (2, 2048), jnp.float32, 0.0, 0.999994)
        cond_1024 = jax.random.uniform(jax.random.fold_in(_rk, 12), (2, 512), jnp.float32, 0.0, 0.999943)
        return (x, fside_BxS_0, cond_1024)
    x, fside_BxS_0, cond_1024 = _rec_inputs()

    def _L0_cond_setup():
        import jax, jax.numpy as jnp
        import numpy as np
        MU = 0.1
        TOL = 1e-09
        ITERS = 30
        EPS = 1e-12

        def _sinkhorn(M, r, c):
            K = jnp.exp(-M / MU)
            K = K / jnp.maximum(K.sum(axis=(-2, -1), keepdims=True), EPS)
            r_ = r[..., None]
            c_ = c[..., None]
            u0 = r_
            u_prev0 = jnp.ones_like(u0)
            v0 = jnp.zeros_like(c_)

            def step(carry, _):
                u, u_prev, v = carry
                diff = jnp.sqrt(jnp.sum((u - u_prev) ** 2, axis=-1))
                active = jnp.max(diff) > TOL
                v_new = c_ / jnp.maximum(jnp.einsum('bnm,bnk->bmk', K, u), EPS)
                u_new = r_ / jnp.maximum(jnp.einsum('bnm,bmk->bnk', K, v_new), EPS)
                u2 = jnp.where(active, u_new, u)
                v2 = jnp.where(active, v_new, v)
                up2 = jnp.where(active, u, u_prev)
                return ((u2, up2, v2), None)
            (u, _, v), _ = jax.lax.scan(step, (u0, u_prev0, v0), None, length=ITERS + 1)
            P = u * K * jnp.swapaxes(v, -2, -1)
            return P
        key = jax.random.key(seed)
        k1, k2, k3 = jax.random.split(key, 3)
        B, N, Nc = (32, 512, 512)
        M = jax.random.uniform(k1, (B, N, Nc), dtype=jnp.float32)
        r = jax.random.uniform(k2, (B, N), dtype=jnp.float32)
        c = jax.random.uniform(k3, (B, Nc), dtype=jnp.float32)
        return {'M': M, 'r': r, 'c': c}
    _L0_cond_all = _L0_cond_setup()
    _L0_cond_in = {k: v for k, v in _L0_cond_all.items() if k in ()}
    del _L0_cond_all

    def _L1_cond_setup():
        import jax, jax.numpy as jnp
        import numpy as np
        import math
        D = 512
        H = 512
        key = jax.random.key(seed)
        k1, k2, k3, k4 = jax.random.split(key, 4)
        x = jax.random.normal(k1, (64, 256, D), dtype=jnp.float32)
        h0 = jax.random.normal(k2, (64, H), dtype=jnp.float32)
        Wx = jax.random.normal(k3, (D, 4 * H), dtype=jnp.float32) / math.sqrt(D)
        Wh = jax.random.normal(k4, (H, 4 * H), dtype=jnp.float32) / math.sqrt(H)
        b = jnp.zeros((4 * H,), dtype=jnp.float32)
        return {'x': x, 'h0': h0, 'Wx': Wx, 'Wh': Wh, 'b': b}
    _L1_cond_all = _L1_cond_setup()
    _L1_cond_in = {k: v for k, v in _L1_cond_all.items() if k in ('Wx', 'Wh', 'b')}
    del _L1_cond_all
    return {'x': x, 'fside_BxS_0': fside_BxS_0, 'cond_1024': cond_1024, 'L1_cond_Wx': _L1_cond_in['Wx'], 'L1_cond_Wh': _L1_cond_in['Wh'], 'L1_cond_b': _L1_cond_in['b']}

def reference(x, fside_BxS_0, cond_1024, L1_cond_Wx, L1_cond_Wh, L1_cond_b):
    import jax
    import jax.numpy as jnp

    def _L0_cond_ref(M, r, c):
        import jax, jax.numpy as jnp
        import numpy as np
        MU = 0.1
        TOL = 1e-09
        ITERS = 30
        EPS = 1e-12

        def _sinkhorn(M, r, c):
            K = jnp.exp(-M / MU)
            K = K / jnp.maximum(K.sum(axis=(-2, -1), keepdims=True), EPS)
            r_ = r[..., None]
            c_ = c[..., None]
            u0 = r_
            u_prev0 = jnp.ones_like(u0)
            v0 = jnp.zeros_like(c_)

            def step(carry, _):
                u, u_prev, v = carry
                diff = jnp.sqrt(jnp.sum((u - u_prev) ** 2, axis=-1))
                active = jnp.max(diff) > TOL
                v_new = c_ / jnp.maximum(jnp.einsum('bnm,bnk->bmk', K, u), EPS)
                u_new = r_ / jnp.maximum(jnp.einsum('bnm,bmk->bnk', K, v_new), EPS)
                u2 = jnp.where(active, u_new, u)
                v2 = jnp.where(active, v_new, v)
                up2 = jnp.where(active, u, u_prev)
                return ((u2, up2, v2), None)
            (u, _, v), _ = jax.lax.scan(step, (u0, u_prev0, v0), None, length=ITERS + 1)
            P = u * K * jnp.swapaxes(v, -2, -1)
            return P
        return _sinkhorn(M, r, c)

    def _L1_cond_ref(x, h0, Wx, Wh, b):
        import jax, jax.numpy as jnp
        import numpy as np
        import math
        D = 512
        H = 512
        xz = jnp.einsum('ntd,dk->ntk', x, Wx) + b
        c0 = jnp.zeros_like(h0)

        def step(carry, xz_t):
            prev_h, prev_c = carry
            z = xz_t + prev_h @ Wh
            ai, af, ao, ag = jnp.split(z, 4, axis=1)
            i = jax.nn.sigmoid(ai)
            f = jax.nn.sigmoid(af)
            o = jax.nn.sigmoid(ao)
            g = jnp.tanh(ag)
            next_c = f * prev_c + i * g
            next_h = o * jnp.tanh(next_c)
            return ((next_h, next_c), next_h)
        _, hs = jax.lax.scan(step, (h0, c0), jnp.swapaxes(xz, 0, 1))
        return jnp.swapaxes(hs, 0, 1)
    x = x + _L0_cond_ref(x, fside_BxS_0, cond_1024)
    x = x + _L1_cond_ref(x, cond_1024, L1_cond_Wx, L1_cond_Wh, L1_cond_b)
    return x

_drawn_inputs = setup_inputs


def setup_inputs(seed=0):
    import zlib

    import numpy as np

    out = dict(_drawn_inputs(seed))
    spreads = {'L1_cond_b': (0.0, 0.1)}
    factors = {'fside_BxS_0': 8.0, 'cond_1024': 8.0}
    for name, (base, spread) in spreads.items():
        noise = np.random.default_rng([zlib.crc32(name.encode()), seed]).standard_normal(out[name].shape)
        drawn = base * np.exp(spread * noise) if base else spread * noise
        out[name] = jnp.asarray(drawn.astype(out[name].dtype))
    for name, factor in factors.items():
        out[name] = (out[name] * factor).astype(out[name].dtype)
    return out
```

```python
from contextlib import ExitStack

import concourse.bass as bass
from concourse import mybir

ALU = mybir.AluOpType
ACT = mybir.ActivationFunctionType
AX = mybir.AxisListType
F32 = mybir.dt.float32
F32R = mybir.dt.float32r
BF16 = mybir.dt.bfloat16
I32 = mybir.dt.int32

MU = 0.1
TOL = 1e-09
ITERS = 30
EPS = 1e-12
STATE_TOL = 2.0 ** -18


def sinkhorn_lstm(nc: bass.Bass, x: bass.AP, r: bass.AP, c: bass.AP, wx: bass.AP, wh: bass.AP, bias: bass.AP,
                  out: bass.AP):
    B, N, M = x.shape
    P = 128
    CH = P // B
    L = N // CH
    KC = M // P
    H = wh.shape[0]
    G4 = wh.shape[1]
    HB = H // P
    GROUPS = [(0, 8), (8, 16), (16, 24), (24, 28), (28, 32)]
    NG = len(GROUPS)
    LC = 4
    NLC = L // LC
    LOW, FULL, REST = 2, 2, CH - 2
    assert B * CH == P and H == M and G4 == 4 * H and L % 2 == 0

    x_v = x.rearrange("b (c s) m -> (b c) s m", c=CH)
    out_v = out.rearrange("b (c s) m -> (b c) s m", c=CH)
    r_v = r.rearrange("b (c s) -> (b c) s", c=CH)
    c_v = c.rearrange("b (k j) -> (b k) j", j=P)
    wx_v = wx.rearrange("(k p) n -> k p n", p=P)
    wh_v = wh.rearrange("(k p) n -> k p n", p=P)
    xz_dram = nc.dram_tensor("xz_scratch", [L, P, G4], F32, kind="Internal").ap()

    ctx = ExitStack()
    with ctx:
        def sb(name, shape, dt, stack=ctx):
            return stack.enter_context(nc.sbuf_tensor(name, shape, dt))

        def pb(name, shape, dt=F32):
            return ctx.enter_context(nc.psum_tensor(name, shape, dt))

        def sem(name):
            return ctx.enter_context(nc.semaphore(name))

        kx = sb("kx", [P, L, M], F32)
        ident = sb("ident", [P, P], F32)
        batch_ones = sb("batch_ones", [P, P], F32)
        ones = sb("ones", [P, P], F32)
        u_row = sb("u_row", [P, L], F32)
        v_row = sb("v_row", [P, M], F32)

        z = pb("z", [P, 4, 512])
        p_a = pb("p_a", [P, 512])
        p_b = pb("p_b", [P, 512])
        p_s = pb("p_s", [P, 512])
        p_v = pb("p_v", [P, 512])

        with ExitStack() as mem:
            k_hi = sb("k_hi", [P, L, M], F32R, mem)
            k_lo = sb("k_lo", [P, L, M], F32R, mem)
            r_in = sb("r_in", [P, L], F32, mem)
            c_in = sb("c_in", [B * KC, P], F32, mem)
            exp_sum = sb("exp_sum", [P, NLC], F32, mem)
            one_sum = sb("one_sum", [P, 2], F32, mem)
            inv_sum = sb("inv_sum", [P, 1], F32, mem)
            W0 = 64
            r_cols = sb("r_cols", [P, L, B], F32, mem)
            r_act = sb("r_act", [P, L, B], F32, mem)
            u = [sb(f"u{n}", [P, L, B], F32, mem) for n in range(2)]
            u_kept = sb("u_kept", [P, L, B], F32, mem)
            u_new = sb("u_new", [P, L, B], F32, mem)
            u_dif = sb("u_dif", [P, L, B], F32, mem)
            u_parts_all = sb("u_parts", [P, W0 + L * 2 * B], F32R, mem)
            u_parts = u_parts_all[:, W0:].rearrange("p (l h b) -> p l h b", h=2, b=B)
            dif_sq = sb("dif_sq", [P, B], F32, mem)
            dif_max = sb("dif_max", [P, 1], F32, mem)
            active = sb("active", [P, 2], F32, mem)
            c_cols = sb("c_cols", [P, B, KC], F32, mem)
            c_act = sb("c_act", [P, B, KC], F32, mem)
            v = sb("v", [P, B, KC], F32, mem)
            v_kept = sb("v_kept", [P, B, KC], F32, mem)
            v_new = sb("v_new", [P, B, KC], F32, mem)
            v_wide = sb("v_wide", [P, KC, B, CH], F32, mem)
            w_rows_all = sb("w_rows", [P, M], F32, mem)
            pair_sum_all = sb("pair_sum", [P, B], F32, mem)
            own = slice(W0, W0 + 2 * B)
            w_rows, pair_sum = w_rows_all[own, :], pair_sum_all[own, :]
            product_sb = sb("product", [P, 4, M], BF16, mem)
            product = [z[:, n, :] for n in range(4)] + [product_sb[:, n, :] for n in range(4)]
            kv = sb("kv", [P, L], F32, mem)
            kv_max = sb("kv_max", [P, L], F32, mem)
            kv_inv = sb("kv_inv", [P, L], F32, mem)
            w_max = sb("w_max", [P, B, KC], F32, mem)
            w_inv = sb("w_inv", [P, B, KC], F32, mem)

            p_w, p_small = p_a, p_s
            w_cols = p_small[:, 0:B * KC].rearrange("p (b k) -> p b k", b=B)
            dif_all = p_b[:, 0:B]
            sum_all = p_b[:, 16:17]
            c_turned = p_small[:, 64:64 + B * KC]

            small_in = sem("small_in")
            x_in = [sem(f"x_in{n}") for n in range(NLC)]
            zeroed = sem("zeroed")
            ident_ready = sem("ident_ready")
            exp_ready = sem("exp_ready")
            summed = sem("summed")
            totalled = sem("totalled")
            inv_ready = sem("inv_ready")
            k_ready = sem("k_ready")
            k_hi_ready = sem("k_hi_ready")
            k_lo_ready = sem("k_lo_ready")
            c_turned_ready = sem("c_turned_ready")
            prepared = sem("prepared")
            parts_hi = sem("parts_hi")
            parts_ready = sem("parts_ready")
            w_ready = sem("w_ready")
            w_copied = sem("w_copied")
            w_cols_ready = sem("w_cols_ready")
            dif_ready = sem("dif_ready")
            dif_squared = sem("dif_squared")
            dif_summed = sem("dif_summed")
            dif_maxed = sem("dif_maxed")
            active_ready = sem("active_ready")
            kept_ready = sem("kept_ready")
            v_new_ready = sem("v_new_ready")
            v_ready = sem("v_ready")
            v_wide_ready = sem("v_wide_ready")
            v_spread = sem("v_spread")
            kv_ready = sem("kv_ready")
            kv_max_ready = sem("kv_max_ready")
            w_max_ready = sem("w_max_ready")
            w_inv_ready = sem("w_inv_ready")
            kv_inv_ready = sem("kv_inv_ready")
            u_new_ready = sem("u_new_ready")
            u_ready = sem("u_ready")

            def flat(t):
                return t[:, :, :].rearrange("p l b -> p (l b)")

            with nc.Block() as block:
                @block.sync
                def _(sp):
                    sp.dma_start(r_in[:], r_v).then_inc(small_in, 16)
                    sp.dma_start(c_in[:], c_v).then_inc(small_in, 16)
                    for n in range(NLC):
                        sp.dma_start(kx[:, n * LC:(n + 1) * LC, :], x_v[:, n * LC:(n + 1) * LC, :]).then_inc(x_in[n], 16)

                @block.gpsimd
                def _(pool):
                    pool.memset(ident[:], 0.0).then_inc(zeroed, 1)
                    pool.wait_ge(zeroed, 1)
                    pool.affine_select(out=ident[:], in_=ident[:], compare_op=ALU.not_equal, fill=1.0, base=0,
                                       pattern=[[-1, P]], channel_multiplier=1).then_inc(ident_ready, 1)

                @block.scalar
                def _(act):
                    for n in range(NLC):
                        act.wait_ge(x_in[n], 16)
                        k = kx[:, n * LC:(n + 1) * LC, :]
                        nc.scalar.activation(k, k, ACT.Exp, scale=-1.0 / MU,
                                             accum_out=exp_sum[:, n:n + 1]).then_inc(exp_ready, 1)
                    for n in range(NLC):
                        act.wait_ge(k_ready, n + 1)
                        nc.scalar.copy(k_hi[:, n * LC:(n + 1) * LC, :],
                                       kx[:, n * LC:(n + 1) * LC, :]).then_inc(k_hi_ready, 1)

                    def iteration(it):
                        act.wait_ge(w_ready, it + 1)
                        nc.scalar.copy(w_rows, p_w[own, :]).then_inc(w_copied, 1)

                    iteration(0)
                    with act.Fori(0, ITERS) as it:
                        iteration(it + 1)
                    act.wait_ge(parts_ready, NG * (ITERS + 2))
                    nc.scalar.copy(v_row[:], p_v[:])

                @block.vector
                def _(dve):
                    dve.memset(batch_ones[:], 0.0).then_inc(prepared, 1)
                    dve.memset(flat(r_cols), 0.0).then_inc(prepared, 1)
                    dve.memset(flat(u[1]), 0.0).then_inc(prepared, 1)
                    dve.memset(v[:], 0.0).then_inc(prepared, 1)
                    dve.memset(ones[:], 1.0).then_inc(prepared, 1)
                    dve.memset(u_parts_all[:, 0:W0].bitcast(F32), 0.0).then_inc(prepared, 1)
                    dve.wait_ge(prepared, 6)
                    dve.wait_ge(small_in, 32)
                    for b in range(B):
                        rows = slice(b * CH, (b + 1) * CH)
                        dve.memset(batch_ones[rows, rows], 1.0).then_inc(prepared, 1)
                        dve.memset(u[1][rows, :, b], 1.0).then_inc(prepared, 1)
                        dve.tensor_copy(r_cols[rows, :, b], r_in[rows, :]).then_inc(prepared, 1)
                    dve.wait_ge(ident_ready, 1)
                    dve.tensor_tensor(pair_sum, ident[own, W0:W0 + B], ident[own, W0 + B:W0 + 2 * B],
                                      ALU.add).then_inc(prepared, 1)
                    dve.wait_ge(prepared, 6 + 3 * B + 1)
                    dve.tensor_copy(flat(u[0]), flat(r_cols)).then_inc(prepared, 1)
                    dve.wait_ge(c_turned_ready, 1)
                    dve.tensor_copy(c_cols[:, :, :].rearrange("p b k -> p (b k)"), c_turned).then_inc(prepared, 1)
                    dve.wait_ge(prepared, 6 + 3 * B + 3)
                    dve.wait_ge(exp_ready, NLC)
                    dve.tensor_reduce(one_sum[:, 0:1], exp_sum[:], AX.X, ALU.add).then_inc(summed, 1)
                    dve.wait_ge(totalled, 1)
                    dve.tensor_scalar(one_sum[:, 1:2], sum_all, EPS, None, ALU.max).then_inc(inv_ready, 1)
                    dve.wait_ge(inv_ready, 1)
                    dve.reciprocal(inv_sum[:], one_sum[:, 1:2]).then_inc(inv_ready, 1)
                    dve.wait_ge(inv_ready, 2)
                    for n in range(NLC):
                        k = kx[:, n * LC:(n + 1) * LC, :]
                        dve.tensor_scalar(k, k, inv_sum[:, 0:1], None, ALU.mult).then_inc(k_ready, 1)
                    for n in range(NLC):
                        sl = slice(n * LC, (n + 1) * LC)
                        dve.wait_ge(k_hi_ready, n + 1)
                        dve.tensor_tensor(k_lo[:, sl, :], kx[:, sl, :], k_hi[:, sl, :].bitcast(F32),
                                          ALU.subtract).then_inc(k_lo_ready, 1)

                    def split_u(un, a, b):
                        dve.tensor_copy(u_parts[:, a:b, 0, :], un[:, a:b, :]).then_inc(parts_hi, 1)

                    def split_lo(un, a, b):
                        dve.tensor_tensor(u_parts[:, a:b, 1, :], un[:, a:b, :], u_parts[:, a:b, 0, :].bitcast(F32),
                                          ALU.subtract).then_inc(parts_ready, 1)

                    for g, (a, b) in enumerate(GROUPS):
                        split_u(u[0], a, b)
                        dve.wait_ge(parts_hi, g + 1)
                        split_lo(u[0], a, b)

                    def iteration(it, cur):
                        un, up = u[cur], u[1 - cur]
                        dve.tensor_tensor(flat(u_dif), flat(un), flat(up), ALU.subtract).then_inc(dif_ready, 1)
                        dve.wait_ge(dif_ready, it + 1)
                        for b in range(B):
                            dve.tensor_tensor_reduce(u_new[:, :, b], u_dif[:, :, b], u_dif[:, :, b], 1.0, 0.0, ALU.mult,
                                                     ALU.add, dif_sq[:, b:b + 1]).then_inc(dif_squared, 1)
                        dve.wait_ge(dif_summed, it + 1)
                        dve.tensor_reduce(dif_max[:], dif_all, AX.X, ALU.max).then_inc(dif_maxed, 1)
                        dve.wait_ge(dif_maxed, it + 1)
                        dve.tensor_scalar(active[:, 0:1], dif_max[:], TOL * TOL, None, ALU.is_gt).then_inc(active_ready, 1)
                        dve.tensor_scalar(active[:, 1:2], dif_max[:], TOL * TOL, None, ALU.is_le).then_inc(active_ready, 1)
                        dve.wait_ge(active_ready, 2 * it + 2)
                        dve.tensor_scalar(c_act[:], c_cols[:], active[:, 0:1], None, ALU.mult).then_inc(kept_ready, 1)
                        dve.tensor_scalar(v_kept[:], v[:], active[:, 1:2], None, ALU.mult).then_inc(kept_ready, 1)
                        dve.tensor_scalar(flat(r_act), flat(r_cols), active[:, 0:1], None, ALU.mult).then_inc(kept_ready, 1)
                        dve.tensor_scalar(flat(u_kept), flat(un), active[:, 1:2], None, ALU.mult).then_inc(kept_ready, 1)
                        dve.wait_ge(kept_ready, 4 * it + 4)
                        dve.wait_ge(w_cols_ready, it + 1)
                        dve.tensor_scalar(w_max[:], w_cols, EPS, None, ALU.max).then_inc(w_max_ready, 1)
                        dve.wait_ge(w_max_ready, it + 1)
                        dve.reciprocal(w_inv[:], w_max[:]).then_inc(w_inv_ready, 1)
                        dve.wait_ge(w_inv_ready, it + 1)
                        dve.tensor_tensor(v_new[:], c_act[:], w_inv[:], ALU.mult).then_inc(v_new_ready, 1)
                        dve.wait_ge(v_new_ready, it + 1)
                        dve.tensor_tensor(v[:], v_new[:], v_kept[:], ALU.add).then_inc(v_ready, 1)
                        dve.wait_ge(v_ready, it + 1)
                        dve.tensor_copy(v_wide[:], v[:, :, :].rearrange("p b k -> p k b").unsqueeze(3)
                                        .to_broadcast([P, KC, B, CH])).then_inc(v_wide_ready, 1)
                        dve.wait_ge(v_spread, it + 1)
                        for g, (a, b) in enumerate(GROUPS):
                            for s in range(a, b):
                                last = dve.tensor_tensor_reduce(product[s - a], kx[:, s, :], p_v[:], 1.0, 0.0, ALU.mult,
                                                                ALU.add, kv[:, s:s + 1])
                            last.then_inc(kv_ready, 1)
                            dve.wait_ge(kv_ready, NG * it + g + 1)
                            dve.tensor_scalar(kv_max[:, a:b], kv[:, a:b], EPS, None, ALU.max).then_inc(kv_max_ready, 1)
                            dve.wait_ge(kv_max_ready, NG * it + g + 1)
                            dve.reciprocal(kv_inv[:, a:b], kv_max[:, a:b]).then_inc(kv_inv_ready, 1)
                            dve.wait_ge(kv_inv_ready, NG * it + g + 1)
                            dve.tensor_tensor(u_new[:, a:b, :], r_act[:, a:b, :],
                                              kv_inv[:, a:b].unsqueeze(2).to_broadcast([P, b - a, B]),
                                              ALU.mult).then_inc(u_new_ready, 1)
                            dve.wait_ge(u_new_ready, NG * it + g + 1)
                            dve.tensor_tensor(up[:, a:b, :], u_new[:, a:b, :], u_kept[:, a:b, :],
                                              ALU.add).then_inc(u_ready, 1)
                            dve.wait_ge(u_ready, NG * it + g + 1)
                            split_u(up, a, b)
                            dve.wait_ge(parts_hi, NG * (it + 1) + g + 1)
                            split_lo(up, a, b)

                    iteration(0, 0)
                    with dve.Fori(0, ITERS // 2) as i:
                        iteration(2 * i + 1, 1)
                        iteration(2 * i + 2, 0)
                    dve.tensor_tensor(u_row[:], u[1][:, :, 0], u[1][:, :, 1], ALU.add)

                @block.tensor
                def _(pe):
                    pe.wait_ge(ident_ready, 1)
                    pe.wait_ge(small_in, 32)
                    pe.transpose(c_turned, c_in[:], ident[0:B * KC, 0:B * KC]).then_inc(c_turned_ready, 1)
                    pe.wait_ge(prepared, 6 + 3 * B + 3)
                    pe.wait_ge(summed, 1)
                    pe.matmul(sum_all, batch_ones[:], one_sum[:, 0:1], start=True, stop=True).then_inc(totalled, 1)
                    pe.wait_ge(k_lo_ready, NLC)

                    def iteration(it):
                        for g, (a, b) in enumerate(GROUPS):
                            pe.wait_ge(parts_ready, NG * it + g + 1)
                            for s in range(a, b):
                                parts = u_parts_all[:, s * 2 * B:W0 + (s + 1) * 2 * B]
                                pe.matmul(p_w[0:W0 + 2 * B, :], parts, k_hi[:, s, :], start=(s == 0), stop=False)
                                last = pe.matmul(p_w[0:W0 + 2 * B, :], parts, k_lo[:, s, :], start=False,
                                                 stop=(s == L - 1))
                        last.then_inc(w_ready, 1)
                        pe.wait_ge(dif_squared, B * it + B)
                        pe.matmul(dif_all, ones[:], dif_sq[:], start=True, stop=True).then_inc(dif_summed, 1)
                        pe.wait_ge(w_copied, it + 1)
                        for k in range(KC):
                            last = pe.matmul(w_cols[:, :, k], w_rows[:, k * P:(k + 1) * P], pair_sum,
                                             start=True, stop=True)
                        last.then_inc(w_cols_ready, 1)
                        pe.wait_ge(v_wide_ready, it + 1)
                        for k in range(KC):
                            last = pe.transpose(p_v[:, k * P:(k + 1) * P],
                                                v_wide[:, k, :, :].rearrange("p b c -> p (b c)"), ident[:])
                        last.then_inc(v_spread, 1)

                    iteration(0)
                    with pe.Fori(0, ITERS) as it:
                        iteration(it + 1)

        with ExitStack() as mem:
            w_hi = sb("wx_hi", [P, KC, G4], F32R, mem)
            w_lo = sb("wx_lo", [P, KC, G4], F32R, mem)
            bias_row = sb("bias_row", [P, 4, 4, P], F32, mem)
            x_step = sb("x_step", [P, 2, M], F32, mem)
            p_step = sb("p_step", [P, 2, M], F32, mem)
            x1_step = sb("x1_step", [P, 2, M], F32, mem)
            xt_hi = sb("xt_hi", [P, 2, KC, P], F32R, mem)
            xt_lo = sb("xt_lo", [P, 2, KC, P], F32R, mem)
            xz = sb("xz_out", [P, 2, HB, 4, P], F32, mem)
            x_turn = [p_a[:, :].rearrange("p (k j) -> p k j", k=KC), p_b[:, :].rearrange("p (k j) -> p k j", k=KC)]

            wx_in = [sem(f"wx_in{k}") for k in range(KC)]
            wx_hi_ready = sem("wx_hi_ready")
            wx_ready = sem("wx_ready")
            bias_in = sem("bias_in")
            x_step_in = [sem(f"x_step_in{j}") for j in range(2)]
            p_ready = sem("p_ready")
            x1_ready = sem("x1_ready")
            x1_kept = sem("x1_kept")
            x_turned = sem("x_turned")
            xt_hi_ready = sem("xt_hi_ready")
            xt_ready = sem("xt_ready")
            xz_summed = sem("xz_summed")
            xz_taken = sem("xz_taken")
            xz_out = [sem(f"xz_stored{j}") for j in range(2)]

            with nc.Block() as block:
                @block.sync
                def _(sp):
                    for k in range(KC):
                        if k >= 2:
                            sp.wait_ge(wx_ready, k - 1)
                        sp.dma_start(xz[:, k % 2, :, :, :].rearrange("p b g j -> p (b g j)"),
                                     wx_v[k]).then_inc(wx_in[k], 16)
                    for g in range(4):
                        sp.dma_start(bias_row[:, :, g, :], bias[g * H:(g + 1) * H].rearrange("(b j) -> b j", b=HB)
                                     .partition_broadcast(P)).then_inc(bias_in, 16)
                    for j in range(2):
                        sp.sem_inc(xz_out[j], 16)

                    def load(s, i, j):
                        sp.wait_ge(x1_ready, s + 1)
                        sp.dma_start(x_step[:, j, :], x_v[:, bass.ds(s, 1), :]).then_inc(x_step_in[j], 16)

                    def store(s, i, j):
                        sp.wait_ge(xz_taken, 4 * s + 8)
                        sp.dma_start(xz_dram[bass.ds(s, 1), :, :].rearrange("s p n -> p (s n)"),
                                     xz[:, j, :, :, :].rearrange("p b g j -> p (b g j)")).then_inc(xz_out[j], 16)

                    for j in range(2):
                        load(j, 0, j)
                    with sp.Fori(0, L // 2 - 1) as i:
                        for j in range(2):
                            load(2 * i + j + 2, i + 1, j)
                            store(2 * i + j, i, j)
                    for j in range(2):
                        store(L - 2 + j, L // 2 - 1, j)
                        sp.wait_ge(xz_out[j], 16 * (L // 2 + 1))

                @block.gpsimd
                def _(pool):
                    pool.sem_inc(x1_ready, 2)
                    with pool.Fori(0, L // 2) as i:
                        for j in range(2):
                            s = 2 * i + j
                            pool.wait_ge(p_ready, s + 1)
                            pool.wait_ge(x_step_in[j], 16 * i + 16)
                            pool.wait_ge(x1_kept, s + 1)
                            pool.wait_ge(x_turned, s + 1)
                            pool.tensor_tensor(x1_step[:, j, :], p_step[:, j, :], x_step[:, j, :],
                                               ALU.add).then_inc(x1_ready, 1)

                @block.scalar
                def _(act):
                    act.sem_inc(x1_kept, 2)
                    for k in range(KC):
                        act.wait_ge(wx_in[k], 16)
                        nc.scalar.copy(w_hi[:, k, :], xz[:, k % 2, :, :, :].rearrange("p b g j -> p (b g j)")) \
                            .then_inc(wx_hi_ready, 1)
                    with act.Fori(0, L // 2) as i:
                        for j in range(2):
                            s = 2 * i + j
                            act.wait_ge(x1_ready, s + 3)
                            nc.scalar.copy(kx[:, bass.ds(s, 1), :], x1_step[:, j:j + 1, :]).then_inc(x1_kept, 1)
                            act.wait_ge(x_turned, s + 3)
                            nc.scalar.copy(xt_hi[:, j, :, :], x_turn[j]).then_inc(xt_hi_ready, 1)

                @block.vector
                def _(dve):
                    def form_p(s, j):
                        dve.wait_ge(x1_ready, s + 1)
                        dve.scalar_tensor_tensor(out=p_step[:, j:j + 1, :], in0=kx[:, bass.ds(s, 1), :],
                                                 scalar=u_row[:, bass.ds(s, 1)],
                                                 in1=v_row[:, :].unsqueeze(1), op0=ALU.mult,
                                                 op1=ALU.mult).then_inc(p_ready, 1)

                    def split_x(s, j):
                        dve.wait_ge(xt_hi_ready, s + 1)
                        dve.tensor_tensor(xt_lo[:, j, :, :], x_turn[j], xt_hi[:, j, :, :].bitcast(F32),
                                          ALU.subtract).then_inc(xt_ready, 1)

                    def take(s, i, j):
                        dve.wait_ge(xz_out[j], 16 * i + 16)
                        for b in range(HB):
                            dve.wait_ge(xz_summed, 4 * s + b + 1)
                            dve.tensor_tensor(xz[:, j, b, :, :], z[:, b, :].rearrange("p (g j) -> p g j", g=4),
                                              bias_row[:, b, :, :], ALU.add).then_inc(xz_taken, 1)

                    for j in range(2):
                        form_p(j, j)
                    for k in range(KC):
                        dve.wait_ge(wx_hi_ready, k + 1)
                        dve.tensor_tensor(w_lo[:, k, :], xz[:, k % 2, :, :, :].rearrange("p b g j -> p (b g j)"),
                                          w_hi[:, k, :].bitcast(F32), ALU.subtract).then_inc(wx_ready, 1)
                    split_x(0, 0)
                    dve.wait_ge(wx_ready, KC)
                    dve.wait_ge(bias_in, 64)
                    with dve.Fori(0, L // 2 - 1) as i:
                        for j in range(2):
                            s = 2 * i + j
                            form_p(s + 2, j)
                            split_x(s + 1, 1 - j)
                            take(s, i, j)
                    split_x(L - 1, 1)
                    for j in range(2):
                        take(L - 2 + j, L // 2 - 1, j)

                @block.tensor
                def _(pe):
                    pe.sem_inc(x_turned, 2)
                    pe.sem_inc(xz_taken, 4)

                    def turn(s, j):
                        pe.wait_ge(x1_ready, s + 3)
                        for k in range(KC):
                            last = pe.transpose(x_turn[j][:, k, :], x1_step[:, j, k * P:(k + 1) * P], ident[:])
                        last.then_inc(x_turned, 1)

                    def project(s, j):
                        pe.wait_ge(xt_ready, s + 1)
                        for b in range(HB):
                            pe.wait_ge(xz_taken, 4 * s + b + 1)
                            for k in range(KC):
                                hi = w_hi[:, k, :].rearrange("p (g b j) -> p b g j", g=4, b=HB)[:, b]
                                lo = w_lo[:, k, :].rearrange("p (g b j) -> p b g j", g=4, b=HB)[:, b]
                                pe.matmul(z[:, b, :], xt_hi[:, j, k, :], hi, start=(k == 0), stop=False)
                                pe.matmul(z[:, b, :], xt_hi[:, j, k, :], lo, start=False, stop=False)
                                last = pe.matmul(z[:, b, :], xt_lo[:, j, k, :], hi, start=False, stop=(k == KC - 1))
                            last.then_inc(xz_summed, 1)

                    turn(0, 0)
                    pe.wait_ge(wx_ready, KC)
                    with pe.Fori(0, L // 2 - 1) as i:
                        for j in range(2):
                            turn(2 * i + j + 1, 1 - j)
                            project(2 * i + j, j)
                    turn(L - 1, 1)
                    for j in range(2):
                        project(L - 2 + j, j)

        with ExitStack() as mem:
            w_hi = sb("wh_hi", [P, HB, G4], F32R, mem)
            w_lo = sb("wh_lo", [P, HB, G4], F32R, mem)
            xz = sb("xz_in", [P, 2, HB, 4, P], F32, mem)
            pre = sb("pre", [P, HB, 4, P], F32, mem)
            gates = sb("gates", [P, HB, 4, P], F32, mem)
            h = sb("h", [P, HB, P], F32, mem)
            cell = sb("cell", [P, HB, P], F32, mem)
            kept = sb("kept", [P, HB, P], F32, mem)
            added = sb("added", [P, HB, P], F32, mem)
            squashed = sb("squashed", [P, HB, P], F32, mem)
            ht_hi = sb("ht_hi", [P, HB, P], F32R, mem)
            ht_lo = sb("ht_lo", [P, HB, P], F32R, mem)
            h_start = sb("h_start", [P, 2, H], F32, mem)
            c_start = sb("c_start", [P, 2, H], F32, mem)
            y = sb("y", [P, 2, H], F32, mem)
            moved_sq = sb("moved_sq", [P, 2], F32, mem)
            moved_max = sb("moved_max", [P, 1], F32, mem)
            settled = sb("settled", [P, 1], F32, mem)
            settled_rows = sb("settled_rows", [1, 1], I32, mem)
            h_turn = [bank[:, 0:P] for bank in (p_a, p_b, p_s, p_v)]
            settled_sum = p_s[0:1, 0:1]

            wh_in = [sem(f"wh_in{k}") for k in range(HB)]
            wh_hi_ready = sem("wh_hi_ready")
            wh_ready = sem("wh_ready")
            cleared = sem("cleared")
            first_in = sem("first_in")
            shifted = sem("shifted")
            restarted = sem("restarted")
            moved = sem("moved")
            settled_ready = sem("settled_ready")
            settled_summed = sem("settled_summed")
            flag_ready = sem("flag_ready")

            class Phase:

                def __init__(self, name, before, count, full):
                    self.before, self.count, self.full = before, count, full
                    self.xz_in = [sem(f"{name}_xz_in{j}") for j in range(2)]
                    self.h_turned = sem(f"{name}_h_turned")
                    self.ht_hi_ready = sem(f"{name}_ht_hi_ready")
                    self.ht_lo_ready = sem(f"{name}_ht_lo_ready")
                    self.summed = sem(f"{name}_summed")
                    self.pre_ready = sem(f"{name}_pre_ready")
                    self.gates_ready = sem(f"{name}_gates_ready")
                    self.kept_ready = sem(f"{name}_kept_ready")
                    self.added_ready = sem(f"{name}_added_ready")
                    self.cell_ready = sem(f"{name}_cell_ready")
                    self.squashed_ready = sem(f"{name}_squashed_ready")
                    self.h_ready = sem(f"{name}_h_ready")
                    self.y_ready = sem(f"{name}_y_ready")
                    self.y_out = [sem(f"{name}_y_stored{j}") for j in range(2)]

            low = Phase("low", 0, LOW, False)
            full = Phase("full", LOW, FULL, True)
            rest = Phase("rest", LOW + FULL, REST, True)

            def run(eng, ph, step, end=None):
                with eng.Fori(0, ph.count) as p:
                    with eng.Fori(0, L // 2) as i:
                        for j in range(2):
                            step(ph, p, p * (L // 2) + i, 2 * i + j, j)
                    if end:
                        end(ph, p)

            def unsettled(eng):
                eng.wait_ge(flag_ready, 1)
                rows = eng.value_load(settled_rows[0:1, 0:1], min_val=0, max_val=P)
                return eng.If(rows < P)

            with nc.Block() as block:
                @block.sync
                def _(sp):
                    for k in range(HB):
                        if k >= 2:
                            sp.wait_ge(wh_ready, k - 1)
                        sp.dma_start(xz[:, k % 2, :, :, :].rearrange("p b g j -> p (b g j)"),
                                     wh_v[k]).then_inc(wh_in[k], 16)
                    sp.wait_ge(cleared, 4)
                    for b in range(B):
                        row = slice(b * CH, b * CH + 1)
                        sp.dma_start(h[row, :, :].rearrange("p b j -> p (b j)"), c[b:b + 1, :]).then_inc(first_in, 16)
                        for n in range(2):
                            sp.dma_start(h_start[row, n, :], c[b:b + 1, :]).then_inc(first_in, 16)
                    sp.wait_ge(wh_ready, HB)

                    def load(ph, n, s, j):
                        sp.wait_ge(ph.pre_ready, 8 * n + 4 * j + 4)
                        sp.dma_start(xz[:, j, :, :, :].rearrange("p b g j -> p (b g j)"),
                                     xz_dram[bass.ds(s, 1), :, :].rearrange("s p n -> p (s n)")) \
                            .then_inc(ph.xz_in[j], 16)

                    def store(ph, n, s, j):
                        sp.wait_ge(ph.y_ready, 2 * n + j + 2)
                        sp.dma_start(out_v[:, bass.ds(s, 1), :], y[:, j:j + 1, :]).then_inc(ph.y_out[j], 16)

                    def passes(ph, slot_of):
                        with sp.Fori(0, ph.count) as p:
                            first = p * (L // 2)
                            for j in range(2):
                                load(ph, first, j, j)
                            with sp.Fori(0, L // 2 - 1) as i:
                                for j in range(2):
                                    if ph.full:
                                        store(ph, first + i, 2 * i + j, j)
                                    load(ph, first + i + 1, 2 * i + j + 2, j)
                            if ph.full:
                                for j in range(2):
                                    store(ph, first + L // 2 - 1, L - 2 + j, j)
                            sp.wait_ge(ph.h_ready, (4 * L + 4) * p + 4 * L + 4)
                            slot = slot_of(p)
                            for b in range(B):
                                a = b * CH
                                for ends, start in ((h, h_start), (cell, c_start)):
                                    sp.dma_start(start[a + 1:a + CH, slot, :],
                                                 ends[a:a + CH - 1, :, :].rearrange("p b j -> p (b j)").unsqueeze(1)) \
                                        .then_inc(shifted, 16)
                        if ph.full:
                            for j in range(2):
                                sp.wait_ge(ph.y_out[j], 16 * (ph.count * (L // 2) + 1))

                    passes(low, lambda p: bass.ds(p, 1))
                    passes(full, lambda p: bass.ds(p, 1))
                    with unsettled(sp):
                        passes(rest, lambda p: slice(0, 1))

                @block.gpsimd
                def _(pool):
                    pool.memset(h[:], 0.0).then_inc(cleared, 1)
                    pool.memset(cell[:], 0.0).then_inc(cleared, 1)
                    pool.memset(h_start[:], 0.0).then_inc(cleared, 1)
                    pool.memset(c_start[:], 0.0).then_inc(cleared, 1)

                    def step(ph, p, n, s, j):
                        for b in range(HB):
                            pool.wait_ge(ph.gates_ready, 8 * n + 4 * j + b + 1)
                            pool.tensor_tensor(added[:, b, :], gates[:, b, 0, :], gates[:, b, 3, :],
                                               ALU.mult).then_inc(ph.added_ready, 1)
                        if ph.full:
                            pool.wait_ge(ph.h_ready, 8 * n + 4 * j + 4 * p + 8)
                            pool.wait_ge(ph.y_out[j], 16 * n + 16)
                            pool.tensor_tensor(y[:, j:j + 1, :], kx[:, bass.ds(s, 1), :],
                                               h[:, :, :].rearrange("p b j -> p (b j)").unsqueeze(1),
                                               ALU.add).then_inc(ph.y_ready, 1)

                    run(pool, low, step)
                    run(pool, full, step)
                    with unsettled(pool):
                        run(pool, rest, step)

                @block.scalar
                def _(act):
                    for k in range(HB):
                        act.wait_ge(wh_in[k], 16)
                        nc.scalar.copy(w_hi[:, k, :], xz[:, k % 2, :, :, :].rearrange("p b g j -> p (b g j)")) \
                            .then_inc(wh_hi_ready, 1)

                    def step(ph, p, n, s, j):
                        first = 8 * n + 4 * j
                        for k in range(HB):
                            act.wait_ge(ph.h_turned, first + k + 1)
                            nc.scalar.copy(ht_hi[:, k, :], h_turn[k]).then_inc(ph.ht_hi_ready, 1)

                        def open_gates(b):
                            act.wait_ge(ph.pre_ready, first + b + 9)
                            nc.scalar.activation(gates[:, b, 0:3, :], pre[:, b, 0:3, :], ACT.Sigmoid)
                            nc.scalar.activation(gates[:, b, 3, :], pre[:, b, 3, :],
                                                 ACT.Tanh).then_inc(ph.gates_ready, 1)

                        def squash(b):
                            act.wait_ge(ph.cell_ready, first + b + 1)
                            nc.scalar.activation(squashed[:, b, :], cell[:, b, :],
                                                 ACT.Tanh).then_inc(ph.squashed_ready, 1)

                        open_gates(0)
                        for b in range(1, HB):
                            open_gates(b)
                            squash(b - 1)
                        squash(HB - 1)

                    run(act, low, step)
                    run(act, full, step)
                    with unsettled(act):
                        run(act, rest, step)

                @block.vector
                def _(dve):
                    for k in range(HB):
                        dve.wait_ge(wh_hi_ready, k + 1)
                        dve.tensor_tensor(w_lo[:, k, :], xz[:, k % 2, :, :, :].rearrange("p b g j -> p (b g j)"),
                                          w_hi[:, k, :].bitcast(F32), ALU.subtract).then_inc(wh_ready, 1)

                    def step(ph, p, n, s, j):
                        first = 8 * n + 4 * j
                        if ph.full:
                            for k in range(HB):
                                dve.wait_ge(ph.ht_hi_ready, first + k + 1)
                                dve.tensor_tensor(ht_lo[:, k, :], h_turn[k], ht_hi[:, k, :].bitcast(F32),
                                                  ALU.subtract).then_inc(ph.ht_lo_ready, 1)

                        def add_input(b):
                            if b == 0:
                                dve.wait_ge(ph.xz_in[j], 16 * n + 16)
                            dve.wait_ge(ph.summed, first + b + 1)
                            dve.tensor_tensor(pre[:, b, :, :], z[:, b, :].rearrange("p (g j) -> p g j", g=4),
                                              xz[:, j, b, :, :], ALU.add).then_inc(ph.pre_ready, 1)

                        def update_cell(b):
                            dve.wait_ge(ph.gates_ready, first + b + 1)
                            dve.tensor_tensor(kept[:, b, :], gates[:, b, 1, :], cell[:, b, :],
                                              ALU.mult).then_inc(ph.kept_ready, 1)
                            dve.wait_ge(ph.kept_ready, first + b + 1)
                            dve.wait_ge(ph.added_ready, first + b + 1)
                            dve.tensor_tensor(cell[:, b, :], kept[:, b, :], added[:, b, :],
                                              ALU.add).then_inc(ph.cell_ready, 1)

                        def form_h(b):
                            dve.wait_ge(ph.squashed_ready, first + b + 1)
                            if ph.full and b == 0:
                                dve.wait_ge(ph.y_ready, 2 * n + j + 1)
                            dve.tensor_tensor(h[:, b, :], gates[:, b, 2, :], squashed[:, b, :],
                                              ALU.mult).then_inc(ph.h_ready, 1)

                        add_input(0)
                        for b in range(1, HB):
                            add_input(b)
                            update_cell(b - 1)
                            if b >= 2:
                                form_h(b - 2)
                        update_cell(HB - 1)
                        form_h(HB - 2)
                        form_h(HB - 1)

                    def restart(slot_of):
                        def end(ph, p):
                            dve.wait_ge(shifted, 64 * p + 64 * (ph.before + 1))
                            if ph.full:
                                dve.wait_ge(ph.y_ready, L * p + L + 1)
                            slot = slot_of(p)
                            dve.tensor_copy(cell[:, :, :].rearrange("p b j -> p (b j)").unsqueeze(1),
                                            c_start[:, slot, :]).then_inc(restarted, 1)
                            dve.tensor_copy(h[:, :, :].rearrange("p b j -> p (b j)").unsqueeze(1),
                                            h_start[:, slot, :]).then_inc(restarted, 1)
                            dve.wait_ge(restarted, 2 * p + 2 * (ph.before + 1))
                            dve.sem_inc(ph.h_ready, 4)
                        return end

                    dve.wait_ge(first_in, 16 * 3 * B)
                    for ph in (low, full, rest):
                        dve.sem_inc(ph.pre_ready, 8)
                        dve.sem_inc(ph.y_ready, 1)
                        for j in range(2):
                            dve.sem_inc(ph.y_out[j], 16)
                    dve.sem_inc(low.h_ready, 4)
                    run(dve, low, step, restart(lambda p: bass.ds(p, 1)))
                    dve.sem_inc(full.h_ready, 4)
                    run(dve, full, step, restart(lambda p: bass.ds(p, 1)))

                    for n, start in enumerate((h_start, c_start)):
                        dve.tensor_tensor(pre[:, n, :, :].rearrange("p g j -> p (g j)"), start[:, 1, :],
                                          start[:, 0, :], ALU.subtract).then_inc(moved, 1)
                        dve.wait_ge(moved, 2 * n + 1)
                        dif = pre[:, n, :, :].rearrange("p g j -> p (g j)")
                        dve.tensor_tensor_reduce(gates[:, n, :, :].rearrange("p g j -> p (g j)"), dif, dif, 1.0, 0.0,
                                                 ALU.mult, ALU.max, moved_sq[:, n:n + 1]).then_inc(moved, 1)
                    dve.wait_ge(moved, 4)
                    dve.tensor_reduce(moved_max[:], moved_sq[:], AX.X, ALU.max).then_inc(moved, 1)
                    dve.wait_ge(moved, 5)
                    dve.tensor_scalar(settled[:], moved_max[:], STATE_TOL * STATE_TOL, None,
                                      ALU.is_le).then_inc(settled_ready, 1)
                    dve.wait_ge(settled_summed, 1)
                    dve.tensor_copy(settled_rows[:], settled_sum).then_inc(flag_ready, 1)
                    with unsettled(dve):
                        dve.sem_inc(rest.h_ready, 4)
                        run(dve, rest, step, restart(lambda p: slice(0, 1)))

                @block.tensor
                def _(pe):
                    pe.wait_ge(wh_ready, HB)

                    def step(ph, p, n, s, j):
                        first = 8 * n + 4 * j
                        for k in range(HB):
                            pe.wait_ge(ph.h_ready, first + 4 * p + k + 1)
                            pe.transpose(h_turn[k], h[:, k, :], ident[:]).then_inc(ph.h_turned, 1)
                            pe.wait_ge(ph.ht_lo_ready if ph.full else ph.ht_hi_ready, first + k + 1)
                            for b in range(HB):
                                if k == 0:
                                    pe.wait_ge(ph.pre_ready, first + b + 5)
                                hi = w_hi[:, k, :].rearrange("p (g b j) -> p b g j", g=4, b=HB)[:, b]
                                lo = w_lo[:, k, :].rearrange("p (g b j) -> p b g j", g=4, b=HB)[:, b]
                                ends = k == HB - 1
                                last = pe.matmul(z[:, b, :], ht_hi[:, k, :], hi, start=(k == 0),
                                                 stop=ends and not ph.full)
                                if ph.full:
                                    pe.matmul(z[:, b, :], ht_hi[:, k, :], lo, start=False, stop=False)
                                    last = pe.matmul(z[:, b, :], ht_lo[:, k, :], hi, start=False, stop=ends)
                                if ends:
                                    last.then_inc(ph.summed, 1)

                    run(pe, low, step)
                    run(pe, full, step)
                    pe.wait_ge(settled_ready, 1)
                    pe.matmul(settled_sum, settled[:], ones[:, 0:1], start=True, stop=True).then_inc(settled_summed, 1)
                    with unsettled(pe):
                        run(pe, rest, step)


_INS = ['x', 'fside_BxS_0', 'cond_1024', 'L1_cond_Wx', 'L1_cond_Wh', 'L1_cond_b']
_OUTS = [((2, 2048, 512), 'float32')]


def kernel(**inputs):
    import numpy as _np
    import concourse.bacc as _bacc
    from concourse import mybir as _mybir
    from concourse.bass_utils import run_bass_kernel_spmd as _run

    nc = _bacc.Bacc("TRN2", target_bir_lowering=False, num_devices=1)
    arrays, args = {}, []
    for name in _INS:
        a = _np.ascontiguousarray(inputs[name])
        arrays[f"in_{name}_dram"] = a
        args.append(nc.dram_tensor(f"in_{name}_dram", a.shape, _mybir.dt.from_np(a.dtype), kind="ExternalInput").ap())
    for i, (shape, dtype) in enumerate(_OUTS):
        dt = _mybir.dt.from_np(_np.dtype(dtype))
        args.append(nc.dram_tensor(f"out_{i}_dram", shape, dt, kind="ExternalOutput").ap())
    sinkhorn_lstm(nc, *args)
    r = _run(nc, [arrays], core_ids=[0])
    return r.results[0]["out_0_dram"]
```

```python
from contextlib import ExitStack

import concourse.bass as bass
import numpy as np
from concourse import mybir

ALU = mybir.AluOpType
ACT = mybir.ActivationFunctionType
AX = mybir.AxisListType
F32 = mybir.dt.float32
F32R = mybir.dt.float32r
BF16 = mybir.dt.bfloat16
I32 = mybir.dt.int32

MU = 0.1
TOL = 1e-09
ITERS = 30
EPS = 1e-12
INV_EPS = float(np.float32(1) / np.float32(EPS))
STATE_TOL = 2.0 ** -18


def sinkhorn_lstm(nc: bass.Bass, x: bass.AP, r: bass.AP, c: bass.AP, wx: bass.AP, wh: bass.AP, bias: bass.AP,
                  out: bass.AP):
    B, N, M = x.shape
    P = 128
    CH = P // B
    L = N // CH
    KC = M // P
    H = wh.shape[0]
    G4 = wh.shape[1]
    HB = H // P
    GROUPS = [(0, 3, 0), (3, 9, 2), (9, 15, 2), (15, 22, 3), (22, 28, 2), (28, 32, 1)]
    NG = len(GROUPS)
    OFF = sum(n for _, _, n in GROUPS)
    OWN = L - OFF
    LC = 4
    NLC = L // LC
    LOW, FULL, REST = 2, 2, CH - 2
    LOW_BY_PE = [2, 3]
    assert B * CH == P and H == M and G4 == 4 * H and L % 2 == 0

    x_v = x.rearrange("b (c s) m -> (b c) s m", c=CH)
    out_v = out.rearrange("b (c s) m -> (b c) s m", c=CH)
    r_v = r.rearrange("b (c s) -> (b c) s", c=CH)
    c_v = c.rearrange("b (k j) -> (b k) j", j=P)
    wx_v = wx.rearrange("(k p) n -> k p n", p=P)
    wh_v = wh.rearrange("(k p) n -> k p n", p=P)
    xz_dram = nc.dram_tensor("xz_scratch", [L, P, G4], F32, kind="Internal").ap()

    ctx = ExitStack()
    with ctx:
        def sb(name, shape, dt, stack=ctx):
            return stack.enter_context(nc.sbuf_tensor(name, shape, dt))

        def pb(name, shape, dt=F32):
            return ctx.enter_context(nc.psum_tensor(name, shape, dt))

        def sem(name):
            return ctx.enter_context(nc.semaphore(name))

        kx = sb("kx", [P, L, M], F32)
        ident = sb("ident", [P, P], F32)
        batch_ones = sb("batch_ones", [P, P], F32)
        ones = sb("ones", [P, P], F32)
        u_row = sb("u_row", [P, L], F32)
        c_cols = sb("c_cols", [P, B, KC], F32)
        v_row = sb("v_row", [P, M], F32)

        z = pb("z", [P, 4, 512])
        p_a = pb("p_a", [P, 512])
        p_b = pb("p_b", [P, 512])
        p_s = pb("p_s", [P, 512])
        p_v = pb("p_v", [P, 512])

        with ExitStack() as mem:
            k_hi = sb("k_hi", [P, L, M], F32R, mem)
            k_lo = sb("k_lo", [P, L, M], F32R, mem)
            r_in = sb("r_in", [P, L], F32, mem)
            c_in = sb("c_in", [B * KC, P], F32, mem)
            exp_sum = sb("exp_sum", [P, NLC], F32, mem)
            one_sum = sb("one_sum", [P, 2], F32, mem)
            inv_sum = sb("inv_sum", [P, 1], F32, mem)
            W0 = 64
            r_cols = sb("r_cols", [P, L, B], F32, mem)
            u = [sb(f"u{n}", [P, L, B], F32, mem) for n in range(2)]
            u_dif = sb("u_dif", [P, L, B], F32, mem)
            u_dif_sq = sb("u_dif_sq", [P, L, B], F32, mem)
            u_parts_all = sb("u_parts", [P, W0 + L * 2 * B], F32R, mem)
            u_parts = u_parts_all[:, W0:].rearrange("p (l h b) -> p l h b", h=2, b=B)
            dif_sq = sb("dif_sq", [P, B], F32, mem)
            dif_max = sb("dif_max", [P, 1], F32, mem)
            active = sb("active", [P, 2], F32, mem)
            c_act = sb("c_act", [P, B, KC], F32, mem)
            v = sb("v", [P, B, KC], F32, mem)
            v_kept = sb("v_kept", [P, B, KC], F32, mem)
            v_new = sb("v_new", [P, B, KC], F32, mem)
            v_wide = sb("v_wide", [P, KC, B, CH], F32, mem)
            w_rows_all = sb("w_rows", [P, M], F32, mem)
            pair_sum_all = sb("pair_sum", [P, B], F32, mem)
            own = slice(W0, W0 + 2 * B)
            w_rows, pair_sum = w_rows_all[own, :], pair_sum_all[own, :]
            product = [z[:, n, :] for n in range(3)]
            off_product = sb("off_product", [P, 2, M], F32, mem)
            p_v_off = z[:, 3, :]
            kv = sb("kv", [P, L], F32, mem)
            kv_inv = sb("kv_inv", [P, L], F32, mem)
            w_inv = sb("w_inv", [P, B, KC], F32, mem)

            p_w, p_small = p_a, p_s
            w_cols = p_small[:, 0:B * KC].rearrange("p (b k) -> p b k", b=B)
            dif_all = p_b[:, 0:B]
            sum_all = p_b[:, 16:17]
            c_turned = p_small[:, 64:64 + B * KC]

            small_in = sem("small_in")
            x_in = [sem(f"x_in{n}") for n in range(NLC)]
            zeroed = sem("zeroed")
            ident_ready = sem("ident_ready")
            exp_ready = sem("exp_ready")
            summed = sem("summed")
            totalled = sem("totalled")
            inv_ready = sem("inv_ready")
            k_ready = sem("k_ready")
            k_hi_ready = sem("k_hi_ready")
            k_lo_ready = sem("k_lo_ready")
            c_turned_ready = sem("c_turned_ready")
            prepared = sem("prepared")
            parts_hi = sem("parts_hi")
            parts_ready = sem("parts_ready")
            w_ready = sem("w_ready")
            w_copied = sem("w_copied")
            w_cols_ready = sem("w_cols_ready")
            dif_ready = sem("dif_ready")
            dif_squared = sem("dif_squared")
            dif_summed = sem("dif_summed")
            dif_maxed = sem("dif_maxed")
            active_ready = sem("active_ready")
            kept_ready = sem("kept_ready")
            v_new_ready = sem("v_new_ready")
            v_ready = sem("v_ready")
            v_wide_ready = sem("v_wide_ready")
            v_spread = sem("v_spread")
            v_spread_off = sem("v_spread_off")
            v_copied = sem("v_copied")
            off_ready = sem("off_ready")
            off_summed = sem("off_summed")
            kv_ready = sem("kv_ready")
            w_inv_ready = sem("w_inv_ready")
            kv_inv_ready = sem("kv_inv_ready")
            u_ready = sem("u_ready")

            def flat(t):
                return t[:, :, :].rearrange("p l b -> p (l b)")

            with nc.Block() as block:
                @block.sync
                def _(sp):
                    sp.dma_start(r_in[:], r_v).then_inc(small_in, 16)
                    sp.dma_start(c_in[:], c_v).then_inc(small_in, 16)
                    for n in range(NLC):
                        sp.dma_start(kx[:, n * LC:(n + 1) * LC, :], x_v[:, n * LC:(n + 1) * LC, :]).then_inc(x_in[n], 16)

                @block.gpsimd
                def _(pool):
                    pool.memset(ident[:], 0.0).then_inc(zeroed, 1)
                    pool.wait_ge(zeroed, 1)
                    pool.affine_select(out=ident[:], in_=ident[:], compare_op=ALU.not_equal, fill=1.0, base=0,
                                       pattern=[[-1, P]], channel_multiplier=1).then_inc(ident_ready, 1)

                    def iteration(it):
                        pool.wait_ge(v_copied, it + 1)
                        n = 0
                        for _, b, off in GROUPS:
                            for s in range(b - off, b):
                                pool.wait_ge(off_summed, OFF * it + n + 1)
                                pool.tensor_tensor(off_product[:, n % 2, :], kx[:, s, :], v_row[:],
                                                   ALU.mult).then_inc(off_ready, 1)
                                n += 1

                    pool.sem_inc(off_summed, 2)
                    pool.wait_ge(k_ready, NLC)
                    iteration(0)
                    with pool.Fori(0, ITERS) as it:
                        iteration(it + 1)

                @block.scalar
                def _(act):
                    for n in range(NLC):
                        act.wait_ge(x_in[n], 16)
                        k = kx[:, n * LC:(n + 1) * LC, :]
                        nc.scalar.activation(k, k, ACT.Exp, scale=-1.0 / MU,
                                             accum_out=exp_sum[:, n:n + 1]).then_inc(exp_ready, 1)
                    for n in range(NLC):
                        act.wait_ge(k_ready, n + 1)
                        nc.scalar.copy(k_hi[:, n * LC:(n + 1) * LC, :],
                                       kx[:, n * LC:(n + 1) * LC, :]).then_inc(k_hi_ready, 1)

                    def iteration(it):
                        act.wait_ge(w_ready, it + 1)
                        nc.scalar.copy(w_rows, p_w[own, :]).then_inc(w_copied, 1)
                        act.wait_ge(v_spread_off, it + 1)
                        nc.scalar.copy(v_row[:], p_v_off).then_inc(v_copied, 1)
                        n = 0
                        for _, b, off in GROUPS:
                            for s in range(b - off, b):
                                act.wait_ge(off_ready, OFF * it + n + 1)
                                nc.scalar.activation(off_product[:, n % 2, :], off_product[:, n % 2, :], ACT.Copy,
                                                     accum_out=kv[:, s:s + 1]).then_inc(off_summed, 1)
                                n += 1

                    iteration(0)
                    with act.Fori(0, ITERS) as it:
                        iteration(it + 1)

                @block.vector
                def _(dve):
                    dve.memset(batch_ones[:], 0.0).then_inc(prepared, 1)
                    dve.memset(flat(r_cols), 0.0).then_inc(prepared, 1)
                    dve.memset(flat(u[1]), 0.0).then_inc(prepared, 1)
                    dve.memset(v[:], 0.0).then_inc(prepared, 1)
                    dve.memset(active[:, 1:2], 1.0).then_inc(prepared, 1)
                    dve.memset(ones[:], 1.0).then_inc(prepared, 1)
                    dve.memset(u_parts_all[:, 0:W0].bitcast(F32), 0.0).then_inc(prepared, 1)
                    dve.wait_ge(prepared, 7)
                    dve.wait_ge(small_in, 32)
                    for b in range(B):
                        rows = slice(b * CH, (b + 1) * CH)
                        dve.memset(batch_ones[rows, rows], 1.0).then_inc(prepared, 1)
                        dve.memset(u[1][rows, :, b], 1.0).then_inc(prepared, 1)
                        dve.tensor_copy(r_cols[rows, :, b], r_in[rows, :]).then_inc(prepared, 1)
                    dve.wait_ge(ident_ready, 1)
                    dve.tensor_tensor(pair_sum, ident[own, W0:W0 + B], ident[own, W0 + B:W0 + 2 * B],
                                      ALU.add).then_inc(prepared, 1)
                    dve.wait_ge(prepared, 7 + 3 * B + 1)
                    dve.tensor_copy(flat(u[0]), flat(r_cols)).then_inc(prepared, 1)
                    dve.wait_ge(c_turned_ready, 1)
                    dve.tensor_copy(c_cols[:, :, :].rearrange("p b k -> p (b k)"), c_turned).then_inc(prepared, 1)
                    dve.wait_ge(prepared, 7 + 3 * B + 3)
                    dve.wait_ge(exp_ready, NLC)
                    dve.tensor_reduce(one_sum[:, 0:1], exp_sum[:], AX.X, ALU.add).then_inc(summed, 1)
                    dve.wait_ge(totalled, 1)
                    dve.tensor_scalar(one_sum[:, 1:2], sum_all, EPS, None, ALU.max).then_inc(inv_ready, 1)
                    dve.wait_ge(inv_ready, 1)
                    dve.reciprocal(inv_sum[:], one_sum[:, 1:2]).then_inc(inv_ready, 1)
                    dve.wait_ge(inv_ready, 2)
                    for n in range(NLC):
                        k = kx[:, n * LC:(n + 1) * LC, :]
                        dve.tensor_scalar(k, k, inv_sum[:, 0:1], None, ALU.mult).then_inc(k_ready, 1)
                    for n in range(NLC):
                        sl = slice(n * LC, (n + 1) * LC)
                        dve.wait_ge(k_hi_ready, n + 1)
                        dve.tensor_tensor(k_lo[:, sl, :], kx[:, sl, :], k_hi[:, sl, :].bitcast(F32),
                                          ALU.subtract).then_inc(k_lo_ready, 1)

                    def split_u(un, a, b):
                        dve.tensor_copy(u_parts[:, a:b, 0, :], un[:, a:b, :]).then_inc(parts_hi, 1)

                    def split_lo(un, a, b):
                        dve.tensor_tensor(u_parts[:, a:b, 1, :], un[:, a:b, :], u_parts[:, a:b, 0, :].bitcast(F32),
                                          ALU.subtract).then_inc(parts_ready, 1)

                    for g, (a, b, off) in enumerate(GROUPS):
                        split_u(u[0], a, b)
                        dve.wait_ge(parts_hi, g + 1)
                        split_lo(u[0], a, b)

                    def iteration(it, cur):
                        un, up = u[cur], u[1 - cur]
                        dve.tensor_tensor(flat(u_dif), flat(un), flat(up), ALU.subtract).then_inc(dif_ready, 1)
                        dve.wait_ge(dif_ready, it + 1)
                        for b in range(B):
                            dve.tensor_tensor_reduce(u_dif_sq[:, :, b], u_dif[:, :, b], u_dif[:, :, b], 1.0, 0.0,
                                                     ALU.mult, ALU.add, dif_sq[:, b:b + 1]).then_inc(dif_squared, 1)
                        dve.wait_ge(dif_summed, it + 1)
                        dve.tensor_reduce(dif_max[:], dif_all, AX.X, ALU.max).then_inc(dif_maxed, 1)
                        dve.wait_ge(dif_maxed, it + 1)
                        now, before = active[:, cur:cur + 1], active[:, 1 - cur:2 - cur]
                        dve.tensor_scalar(now, dif_max[:], TOL * TOL, before, ALU.is_gt, ALU.min).then_inc(active_ready, 1)
                        dve.wait_ge(active_ready, it + 1)
                        dve.tensor_scalar(c_act[:], c_cols[:], now, None, ALU.mult).then_inc(kept_ready, 1)
                        dve.scalar_tensor_tensor(out=v_kept[:], in0=v[:], scalar=now, in1=v[:], op0=ALU.mult,
                                                 op1=ALU.subtract).then_inc(kept_ready, 1)
                        dve.wait_ge(w_cols_ready, it + 1)
                        dve.reciprocal(w_inv[:], w_cols).then_inc(w_inv_ready, 1)
                        dve.wait_ge(w_inv_ready, it + 1)
                        dve.wait_ge(kept_ready, 2 * it + 2)
                        dve.scalar_tensor_tensor(out=v_new[:], in0=w_inv[:], scalar=INV_EPS, in1=c_act[:], op0=ALU.min,
                                                 op1=ALU.mult).then_inc(v_new_ready, 1)
                        dve.wait_ge(v_new_ready, it + 1)

                        def spread(t):
                            return t[:, :, :].rearrange("p b k -> p k b").unsqueeze(3).to_broadcast([P, KC, B, CH])

                        dve.tensor_tensor(v_wide[:], spread(v_new), spread(v_kept), ALU.subtract).then_inc(v_wide_ready, 1)
                        dve.tensor_tensor(v[:], v_new[:], v_kept[:], ALU.subtract).then_inc(v_ready, 1)
                        dve.wait_ge(v_spread, it + 1)
                        n = done = 0
                        for g, (a, b, off) in enumerate(GROUPS):
                            for s in range(a, b - off):
                                if s - a >= len(product):
                                    dve.wait_ge(kv_ready, OWN * it + n + 1 - len(product))
                                dve.tensor_tensor_reduce(product[n % len(product)], kx[:, s, :], p_v[:], 1.0, 0.0,
                                                         ALU.mult, ALU.add, kv[:, s:s + 1]).then_inc(kv_ready, 1)
                                n += 1
                            done += off
                            dve.wait_ge(kv_ready, OWN * it + n)
                            dve.wait_ge(off_summed, OFF * it + done + 2)
                            dve.reciprocal(kv_inv[:, a:b], kv[:, a:b]).then_inc(kv_inv_ready, 1)
                            dve.wait_ge(kv_inv_ready, NG * it + g + 1)
                            inv = kv_inv[:, a:b].unsqueeze(2).to_broadcast([P, b - a, B])
                            dve.scalar_tensor_tensor(out=up[:, a:b, :], in0=inv, scalar=INV_EPS, in1=r_cols[:, a:b, :],
                                                     op0=ALU.min, op1=ALU.mult).then_inc(u_ready, 1)
                            dve.scalar_tensor_tensor(out=u_parts[:, a:b, 0, :], in0=inv, scalar=INV_EPS,
                                                     in1=r_cols[:, a:b, :], op0=ALU.min,
                                                     op1=ALU.mult).then_inc(parts_hi, 1)
                            dve.wait_ge(u_ready, NG * it + g + 1)
                            dve.wait_ge(parts_hi, NG * (it + 1) + g + 1)
                            split_lo(up, a, b)

                    iteration(0, 0)
                    with dve.Fori(0, ITERS // 2) as i:
                        iteration(2 * i + 1, 1)
                        iteration(2 * i + 2, 0)
                    dve.tensor_tensor(u_row[:], u[1][:, :, 0], u[1][:, :, 1], ALU.add)

                @block.tensor
                def _(pe):
                    pe.wait_ge(ident_ready, 1)
                    pe.wait_ge(small_in, 32)
                    pe.transpose(c_turned, c_in[:], ident[0:B * KC, 0:B * KC]).then_inc(c_turned_ready, 1)
                    pe.wait_ge(prepared, 7 + 3 * B + 3)
                    pe.wait_ge(summed, 1)
                    pe.matmul(sum_all, batch_ones[:], one_sum[:, 0:1], start=True, stop=True).then_inc(totalled, 1)
                    pe.wait_ge(k_lo_ready, NLC)

                    def iteration(it):
                        for g, (a, b, off) in enumerate(GROUPS):
                            pe.wait_ge(parts_ready, NG * it + g + 1)
                            for s in range(a, b):
                                parts = u_parts_all[:, s * 2 * B:W0 + (s + 1) * 2 * B]
                                pe.matmul(p_w[0:W0 + 2 * B, :], parts, k_hi[:, s, :], start=(s == 0), stop=False)
                                last = pe.matmul(p_w[0:W0 + 2 * B, :], parts, k_lo[:, s, :], start=False,
                                                 stop=(s == L - 1))
                        last.then_inc(w_ready, 1)
                        pe.wait_ge(dif_squared, B * it + B)
                        pe.matmul(dif_all, ones[:], dif_sq[:], start=True, stop=True).then_inc(dif_summed, 1)
                        pe.wait_ge(w_copied, it + 1)
                        for k in range(KC):
                            last = pe.matmul(w_cols[:, :, k], w_rows[:, k * P:(k + 1) * P], pair_sum,
                                             start=True, stop=True)
                        last.then_inc(w_cols_ready, 1)
                        pe.wait_ge(v_wide_ready, it + 1)
                        for k in range(KC):
                            last = pe.transpose(p_v[:, k * P:(k + 1) * P],
                                                v_wide[:, k, :, :].rearrange("p b c -> p (b c)"), ident[:])
                        last.then_inc(v_spread, 1)
                        for k in range(KC):
                            last = pe.transpose(p_v_off[:, k * P:(k + 1) * P],
                                                v_wide[:, k, :, :].rearrange("p b c -> p (b c)"), ident[:])
                        last.then_inc(v_spread_off, 1)

                    iteration(0)
                    with pe.Fori(0, ITERS) as it:
                        iteration(it + 1)

        with ExitStack() as mem:
            w_hi = sb("wx_hi", [P, KC, G4], F32R, mem)
            w_lo = sb("wx_lo", [P, KC, G4], F32R, mem)
            bias_row = sb("bias_row", [P, 4, 4, P], F32, mem)
            x_step = sb("x_step", [P, 2, M], F32, mem)
            p_step = sb("p_step", [P, 2, M], F32, mem)
            x1_step = sb("x1_step", [P, 2, M], F32, mem)
            xt_hi = sb("xt_hi", [P, 2, KC, P], F32R, mem)
            xt_lo = sb("xt_lo", [P, 2, KC, P], F32R, mem)
            xz = sb("xz_out", [P, 2, HB, 4, P], F32, mem)
            x_turn = [p_a[:, :].rearrange("p (k j) -> p k j", k=KC), p_b[:, :].rearrange("p (k j) -> p k j", k=KC)]

            wx_in = [sem(f"wx_in{k}") for k in range(KC)]
            wx_hi_ready = sem("wx_hi_ready")
            wx_ready = sem("wx_ready")
            bias_in = sem("bias_in")
            x_step_in = [sem(f"x_step_in{j}") for j in range(2)]
            p_ready = sem("p_ready")
            x1_ready = sem("x1_ready")
            x1_kept = sem("x1_kept")
            x_turned = sem("x_turned")
            xt_hi_ready = sem("xt_hi_ready")
            xt_ready = sem("xt_ready")
            xz_summed = sem("xz_summed")
            xz_taken = sem("xz_taken")
            xz_out = [sem(f"xz_stored{j}") for j in range(2)]

            with nc.Block() as block:
                @block.sync
                def _(sp):
                    for k in range(KC):
                        if k >= 2:
                            sp.wait_ge(wx_ready, k - 1)
                        sp.dma_start(xz[:, k % 2, :, :, :].rearrange("p b g j -> p (b g j)"),
                                     wx_v[k]).then_inc(wx_in[k], 16)
                    for g in range(4):
                        sp.dma_start(bias_row[:, :, g, :], bias[g * H:(g + 1) * H].rearrange("(b j) -> b j", b=HB)
                                     .partition_broadcast(P)).then_inc(bias_in, 16)
                    for j in range(2):
                        sp.sem_inc(xz_out[j], 16)

                    def load(s, i, j):
                        sp.wait_ge(x1_ready, s + 1)
                        sp.dma_start(x_step[:, j, :], x_v[:, bass.ds(s, 1), :]).then_inc(x_step_in[j], 16)

                    def store(s, i, j):
                        sp.wait_ge(xz_taken, 4 * s + 8)
                        sp.dma_start(xz_dram[bass.ds(s, 1), :, :].rearrange("s p n -> p (s n)"),
                                     xz[:, j, :, :, :].rearrange("p b g j -> p (b g j)")).then_inc(xz_out[j], 16)

                    for j in range(2):
                        load(j, 0, j)
                    with sp.Fori(0, L // 2 - 1) as i:
                        for j in range(2):
                            load(2 * i + j + 2, i + 1, j)
                            store(2 * i + j, i, j)
                    for j in range(2):
                        store(L - 2 + j, L // 2 - 1, j)
                        sp.wait_ge(xz_out[j], 16 * (L // 2 + 1))

                @block.gpsimd
                def _(pool):
                    pool.sem_inc(x1_ready, 2)
                    with pool.Fori(0, L // 2) as i:
                        for j in range(2):
                            s = 2 * i + j
                            pool.wait_ge(p_ready, s + 1)
                            pool.wait_ge(x_step_in[j], 16 * i + 16)
                            pool.wait_ge(x1_kept, s + 1)
                            pool.wait_ge(x_turned, s + 1)
                            pool.tensor_tensor(x1_step[:, j, :], p_step[:, j, :], x_step[:, j, :],
                                               ALU.add).then_inc(x1_ready, 1)

                @block.scalar
                def _(act):
                    act.sem_inc(x1_kept, 2)
                    for k in range(KC):
                        act.wait_ge(wx_in[k], 16)
                        nc.scalar.copy(w_hi[:, k, :], xz[:, k % 2, :, :, :].rearrange("p b g j -> p (b g j)")) \
                            .then_inc(wx_hi_ready, 1)
                    with act.Fori(0, L // 2) as i:
                        for j in range(2):
                            s = 2 * i + j
                            act.wait_ge(x1_ready, s + 3)
                            nc.scalar.copy(kx[:, bass.ds(s, 1), :], x1_step[:, j:j + 1, :]).then_inc(x1_kept, 1)
                            act.wait_ge(x_turned, s + 3)
                            nc.scalar.copy(xt_hi[:, j, :, :], x_turn[j]).then_inc(xt_hi_ready, 1)

                @block.vector
                def _(dve):
                    def form_p(s, j):
                        dve.wait_ge(x1_ready, s + 1)
                        dve.scalar_tensor_tensor(out=p_step[:, j:j + 1, :], in0=kx[:, bass.ds(s, 1), :],
                                                 scalar=u_row[:, bass.ds(s, 1)],
                                                 in1=v_row[:, :].unsqueeze(1), op0=ALU.mult,
                                                 op1=ALU.mult).then_inc(p_ready, 1)

                    def split_x(s, j):
                        dve.wait_ge(xt_hi_ready, s + 1)
                        dve.tensor_tensor(xt_lo[:, j, :, :], x_turn[j], xt_hi[:, j, :, :].bitcast(F32),
                                          ALU.subtract).then_inc(xt_ready, 1)

                    def take(s, i, j):
                        dve.wait_ge(xz_out[j], 16 * i + 16)
                        for b in range(HB):
                            dve.wait_ge(xz_summed, 4 * s + b + 1)
                            dve.tensor_tensor(xz[:, j, b, :, :], z[:, b, :].rearrange("p (g j) -> p g j", g=4),
                                              bias_row[:, b, :, :], ALU.add).then_inc(xz_taken, 1)

                    for j in range(2):
                        form_p(j, j)
                    for k in range(KC):
                        dve.wait_ge(wx_hi_ready, k + 1)
                        dve.tensor_tensor(w_lo[:, k, :], xz[:, k % 2, :, :, :].rearrange("p b g j -> p (b g j)"),
                                          w_hi[:, k, :].bitcast(F32), ALU.subtract).then_inc(wx_ready, 1)
                    split_x(0, 0)
                    dve.wait_ge(wx_ready, KC)
                    dve.wait_ge(bias_in, 64)
                    with dve.Fori(0, L // 2 - 1) as i:
                        for j in range(2):
                            s = 2 * i + j
                            form_p(s + 2, j)
                            split_x(s + 1, 1 - j)
                            take(s, i, j)
                    split_x(L - 1, 1)
                    for j in range(2):
                        take(L - 2 + j, L // 2 - 1, j)

                @block.tensor
                def _(pe):
                    pe.sem_inc(x_turned, 2)
                    pe.sem_inc(xz_taken, 4)

                    def turn(s, j):
                        pe.wait_ge(x1_ready, s + 3)
                        for k in range(KC):
                            last = pe.transpose(x_turn[j][:, k, :], x1_step[:, j, k * P:(k + 1) * P], ident[:])
                        last.then_inc(x_turned, 1)

                    def project(s, j):
                        pe.wait_ge(xt_ready, s + 1)
                        for b in range(HB):
                            pe.wait_ge(xz_taken, 4 * s + b + 1)
                            for k in range(KC):
                                hi = w_hi[:, k, :].rearrange("p (g b j) -> p b g j", g=4, b=HB)[:, b]
                                lo = w_lo[:, k, :].rearrange("p (g b j) -> p b g j", g=4, b=HB)[:, b]
                                pe.matmul(z[:, b, :], xt_hi[:, j, k, :], hi, start=(k == 0), stop=False)
                                pe.matmul(z[:, b, :], xt_hi[:, j, k, :], lo, start=False, stop=False)
                                last = pe.matmul(z[:, b, :], xt_lo[:, j, k, :], hi, start=False, stop=(k == KC - 1))
                            last.then_inc(xz_summed, 1)

                    turn(0, 0)
                    pe.wait_ge(wx_ready, KC)
                    with pe.Fori(0, L // 2 - 1) as i:
                        for j in range(2):
                            turn(2 * i + j + 1, 1 - j)
                            project(2 * i + j, j)
                    turn(L - 1, 1)
                    for j in range(2):
                        project(L - 2 + j, j)

        with ExitStack() as mem:
            w_hi = sb("wh_hi", [P, HB, G4], F32R, mem)
            w_lo = sb("wh_lo", [P, HB, G4], F32R, mem)
            xz = sb("xz_in", [P, 2, HB, 4, P], F32, mem)
            pre = sb("pre", [P, HB, 4, P], F32, mem)
            gates = sb("gates", [P, HB, 4, P], F32, mem)
            h = sb("h", [P, HB, P], F32, mem)
            cell = sb("cell", [P, HB, P], F32, mem)
            kept = sb("kept", [P, HB, P], F32, mem)
            added = sb("added", [P, HB, P], F32, mem)
            squashed = sb("squashed", [P, HB, P], F32, mem)
            ht_hi = sb("ht_hi", [P, HB, P], F32R, mem)
            ht_lo = sb("ht_lo", [P, HB, P], F32R, mem)
            first_hi = sb("first_hi", [P, B, KC], F32R, mem)
            first_lo = sb("first_lo", [P, B, KC], F32R, mem)
            h_end = sb("h_end", [P, 2, H], F32, mem)
            c_start = sb("c_start", [P, 2, H], F32, mem)
            y = sb("y", [P, 2, H], F32, mem)
            moved_sq = sb("moved_sq", [P, 2], F32, mem)
            moved_max = sb("moved_max", [P, 1], F32, mem)
            settled = sb("settled", [P, 1], F32, mem)
            settled_rows = sb("settled_rows", [1, 1], I32, mem)
            h_turn = [bank[:, 0:P] for bank in (p_a, p_b, p_s, p_v)]
            settled_sum = p_s[0:1, 0:1]

            wh_in = [sem(f"wh_in{k}") for k in range(HB)]
            wh_hi_ready = sem("wh_hi_ready")
            wh_ready = sem("wh_ready")
            cleared = sem("cleared")
            first_split = sem("first_split")
            lows = sem("lows")
            shifted = sem("shifted")
            restarted = sem("restarted")
            moved = sem("moved")
            settled_ready = sem("settled_ready")
            settled_summed = sem("settled_summed")
            flag_ready = sem("flag_ready")

            class Phase:

                def __init__(self, name, before, count, full, by_pe):
                    self.before, self.count, self.full = before, count, full
                    self.by_pe = by_pe
                    self.by_dve = [b for b in range(HB) if b not in by_pe]
                    self.xz_in = [sem(f"{name}_xz_in{j}") for j in range(2)]
                    self.h_turned = sem(f"{name}_h_turned")
                    self.ht_hi_ready = sem(f"{name}_ht_hi_ready")
                    self.ht_lo_ready = sem(f"{name}_ht_lo_ready")
                    self.summed = sem(f"{name}_summed")
                    self.pre_ready = sem(f"{name}_pre_ready")
                    self.gates_ready = sem(f"{name}_gates_ready")
                    self.kept_ready = sem(f"{name}_kept_ready")
                    self.added_ready = sem(f"{name}_added_ready")
                    self.own_added_ready = sem(f"{name}_own_added_ready")
                    self.cell_ready = sem(f"{name}_cell_ready")
                    self.squashed_ready = sem(f"{name}_squashed_ready")
                    self.h_ready = sem(f"{name}_h_ready")
                    self.ended = sem(f"{name}_ended")
                    self.y_ready = sem(f"{name}_y_ready")
                    self.y_out = [sem(f"{name}_y_stored{j}") for j in range(2)]

            low = Phase("low", 0, LOW, False, LOW_BY_PE)
            full = Phase("full", LOW, FULL, True, [])
            rest = Phase("rest", LOW + FULL, REST, True, [])

            def run(eng, ph, step, end=None):
                with eng.Fori(0, ph.count) as p:
                    with eng.Fori(0, L // 2) as i:
                        for j in range(2):
                            step(ph, p, p * (L // 2) + i, 2 * i + j, j)
                    if end:
                        end(ph, p)

            def later(ht, k):
                return ht[:, k, :].rearrange("p (b c) -> p b c", b=B)[:, :, 1:CH]

            def earlier(k):
                return h_turn[k].rearrange("p (b c) -> p b c", b=B)[:, :, 0:CH - 1]

            def unsettled(eng):
                eng.wait_ge(flag_ready, 1)
                rows = eng.value_load(settled_rows[0:1, 0:1], min_val=0, max_val=P)
                return eng.If(rows < P)

            with nc.Block() as block:
                @block.sync
                def _(sp):
                    for k in range(HB):
                        if k >= 2:
                            sp.wait_ge(wh_ready, k - 1)
                        sp.dma_start(xz[:, k % 2, :, :, :].rearrange("p b g j -> p (b g j)"),
                                     wh_v[k]).then_inc(wh_in[k], 16)
                    sp.wait_ge(wh_ready, HB)

                    def load(ph, n, s, j):
                        sp.wait_ge(ph.gates_ready, 8 * n + 4 * j + 4)
                        sp.dma_start(xz[:, j, :, :, :].rearrange("p b g j -> p (b g j)"),
                                     xz_dram[bass.ds(s, 1), :, :].rearrange("s p n -> p (s n)")) \
                            .then_inc(ph.xz_in[j], 16)

                    def store(ph, n, s, j):
                        sp.wait_ge(ph.y_ready, 2 * n + j + 2)
                        sp.dma_start(out_v[:, bass.ds(s, 1), :], y[:, j:j + 1, :]).then_inc(ph.y_out[j], 16)

                    def passes(ph, slot_of):
                        with sp.Fori(0, ph.count) as p:
                            first = p * (L // 2)
                            for j in range(2):
                                load(ph, first, j, j)
                            with sp.Fori(0, L // 2 - 1) as i:
                                for j in range(2):
                                    if ph.full:
                                        store(ph, first + i, 2 * i + j, j)
                                    load(ph, first + i + 1, 2 * i + j + 2, j)
                            if ph.full:
                                for j in range(2):
                                    store(ph, first + L // 2 - 1, L - 2 + j, j)
                            sp.wait_ge(ph.h_ready, (4 * L + 4) * p + 4 * L + 4)
                            slot = slot_of(p)
                            for b in range(B):
                                a = b * CH
                                sp.dma_start(c_start[a + 1:a + CH, slot, :],
                                             cell[a:a + CH - 1, :, :].rearrange("p b j -> p (b j)").unsqueeze(1)) \
                                    .then_inc(shifted, 16)
                        if ph.full:
                            for j in range(2):
                                sp.wait_ge(ph.y_out[j], 16 * (ph.count * (L // 2) + 1))

                    passes(low, lambda p: bass.ds(p, 1))
                    passes(full, lambda p: bass.ds(p, 1))
                    with unsettled(sp):
                        passes(rest, lambda p: slice(0, 1))

                @block.gpsimd
                def _(pool):
                    pool.memset(h[:], 0.0).then_inc(cleared, 1)
                    pool.memset(cell[:], 0.0).then_inc(cleared, 1)
                    pool.memset(c_start[:], 0.0).then_inc(cleared, 1)
                    pool.memset(ht_hi[:, :, :].bitcast(F32), 0.0).then_inc(cleared, 1)
                    pool.memset(ht_lo[:, :, :].bitcast(F32), 0.0).then_inc(cleared, 1)

                    def step(ph, p, n, s, j):
                        if ph.full:
                            for b in range(1, HB):
                                pool.wait_ge(ph.gates_ready, 8 * n + 4 * j + b + 9)
                                pool.tensor_tensor(added[:, b, :], gates[:, b, 0, :], gates[:, b, 3, :],
                                                   ALU.mult).then_inc(ph.added_ready, 1)
                            pool.wait_ge(ph.h_ready, 8 * n + 4 * j + 4 * p + 8)
                            pool.wait_ge(ph.y_out[j], 16 * n + 16)
                            pool.tensor_tensor(y[:, j:j + 1, :], kx[:, bass.ds(s, 1), :],
                                               h[:, :, :].rearrange("p b j -> p (b j)").unsqueeze(1),
                                               ALU.add).then_inc(ph.y_ready, 1)

                    run(pool, low, step)
                    run(pool, full, step)
                    with unsettled(pool):
                        run(pool, rest, step)

                @block.scalar
                def _(act):
                    for k in range(HB):
                        act.wait_ge(wh_in[k], 16)
                        nc.scalar.copy(w_hi[:, k, :], xz[:, k % 2, :, :, :].rearrange("p b g j -> p (b g j)")) \
                            .then_inc(wh_hi_ready, 1)

                    def step(ph, p, n, s, j):
                        first = 8 * n + 4 * j

                        def open_gates(b):
                            if b in ph.by_pe:
                                act.wait_ge(ph.summed, first + b + 1)
                                opened = z[:, b, :].rearrange("p (g j) -> p g j", g=4)
                            else:
                                act.wait_ge(ph.pre_ready, len(ph.by_dve) * (2 * n + j) + ph.by_dve.index(b) + 1)
                                opened = pre[:, b, :, :]
                            nc.scalar.activation(gates[:, b, 0:3, :], opened[:, 0:3, :], ACT.Sigmoid)
                            nc.scalar.activation(gates[:, b, 3, :], opened[:, 3, :],
                                                 ACT.Tanh).then_inc(ph.gates_ready, 1)

                        def squash(b):
                            act.wait_ge(ph.cell_ready, first + b + 1)
                            nc.scalar.activation(squashed[:, b, :], cell[:, b, :],
                                                 ACT.Tanh).then_inc(ph.squashed_ready, 1)

                        def take_hi(b):
                            act.wait_ge(ph.h_turned, first + 4 * p + b + 5)
                            nc.scalar.copy(ht_hi[:, b, :], h_turn[b]).then_inc(ph.ht_hi_ready, 1)

                        open_gates(0)
                        open_gates(1)
                        squash(0)
                        open_gates(2)
                        squash(1)
                        take_hi(0)
                        open_gates(3)
                        take_hi(1)
                        squash(2)
                        take_hi(2)
                        squash(3)
                        take_hi(3)

                    def end(ph, p):
                        act.wait_ge(ph.ended, p + 1)
                        for k in range(HB):
                            nc.scalar.copy(later(ht_hi, k), earlier(k)).then_inc(ph.ht_hi_ready, 1)

                    nc.scalar.preload_act_table_set("sigmoid_and_others")
                    run(act, low, step, end)
                    run(act, full, step, end)
                    with unsettled(act):
                        run(act, rest, step, end)

                @block.vector
                def _(dve):
                    for k in range(HB):
                        dve.wait_ge(wh_hi_ready, k + 1)
                        dve.tensor_tensor(w_lo[:, k, :], xz[:, k % 2, :, :, :].rearrange("p b g j -> p (b g j)"),
                                          w_hi[:, k, :].bitcast(F32), ALU.subtract).then_inc(wh_ready, 1)

                    def step(ph, p, n, s, j):
                        first = 8 * n + 4 * j
                        def add_input(b):
                            if b in ph.by_pe:
                                return
                            if b == 0:
                                dve.wait_ge(ph.xz_in[j], 16 * n + 16)
                            dve.wait_ge(ph.summed, first + b + 1)
                            dve.tensor_tensor(pre[:, b, :, :], z[:, b, :].rearrange("p (g j) -> p g j", g=4),
                                              xz[:, j, b, :, :], ALU.add).then_inc(ph.pre_ready, 1)

                        def update_cell(b):
                            dve.wait_ge(ph.gates_ready, first + b + 9)
                            if b == 0 or not ph.full:
                                dve.tensor_tensor(added[:, b, :], gates[:, b, 0, :], gates[:, b, 3, :],
                                                  ALU.mult).then_inc(ph.own_added_ready, 1)
                            dve.tensor_tensor(kept[:, b, :], gates[:, b, 1, :], cell[:, b, :],
                                              ALU.mult).then_inc(ph.kept_ready, 1)
                            dve.wait_ge(ph.kept_ready, first + b + 1)
                            if not ph.full:
                                dve.wait_ge(ph.own_added_ready, first + b + 1)
                            elif b == 0:
                                dve.wait_ge(ph.own_added_ready, 2 * n + j + 1)
                            else:
                                dve.wait_ge(ph.added_ready, 3 * (2 * n + j) + b)
                            dve.tensor_tensor(cell[:, b, :], kept[:, b, :], added[:, b, :],
                                              ALU.add).then_inc(ph.cell_ready, 1)

                        def form_h(b):
                            dve.wait_ge(ph.squashed_ready, first + b + 1)
                            if ph.full and b == 0:
                                dve.wait_ge(ph.y_ready, 2 * n + j + 1)
                            dve.tensor_tensor(h[:, b, :], gates[:, b, 2, :], squashed[:, b, :],
                                              ALU.mult).then_inc(ph.h_ready, 1)

                        def take_lo(b):
                            if ph.full:
                                dve.wait_ge(ph.ht_hi_ready, first + 4 * p + b + 5)
                                dve.tensor_tensor(ht_lo[:, b, :], h_turn[b], ht_hi[:, b, :].bitcast(F32),
                                                  ALU.subtract).then_inc(ph.ht_lo_ready, 1)

                        add_input(0)
                        add_input(1)
                        update_cell(0)
                        add_input(2)
                        update_cell(1)
                        form_h(0)
                        add_input(3)
                        form_h(1)
                        take_lo(0)
                        update_cell(2)
                        take_lo(1)
                        update_cell(3)
                        form_h(2)
                        form_h(3)
                        take_lo(2)
                        take_lo(3)

                    def restart(slot_of):
                        def end(ph, p):
                            last = 4 * L + (4 * L + 4) * p
                            if ph.full:
                                dve.wait_ge(ph.ht_lo_ready, last + 4)
                            else:
                                dve.wait_ge(ph.ht_hi_ready, last + 4)
                            dve.wait_ge(ph.h_turned, last + 4)
                            dve.tensor_copy(h_end[:, slot_of(p), :].rearrange("p s j -> p (s j)"),
                                            h[:, :, :].rearrange("p b j -> p (b j)")).then_inc(ph.ended, 1)
                            for b in range(HB):
                                dve.wait_ge(ph.ht_hi_ready, last + b + 5)
                                dve.tensor_tensor(later(ht_lo, b), earlier(b), later(ht_hi, b).bitcast(F32),
                                                  ALU.subtract).then_inc(ph.ht_lo_ready if ph.full else lows, 1)
                            restore_first()
                            dve.wait_ge(first_split, 2 + 2 * p + 2 * (ph.before + 2))
                            if ph.full:
                                dve.wait_ge(ph.ht_lo_ready, last + 8)
                            else:
                                dve.wait_ge(lows, 4 * p + 4)
                            dve.sem_inc(ph.h_ready, 4)
                            dve.wait_ge(shifted, 16 * B * p + 16 * B * (ph.before + 1))
                            dve.tensor_copy(cell[:, :, :].rearrange("p b j -> p (b j)"),
                                            c_start[:, slot_of(p), :].rearrange("p s j -> p (s j)")) \
                                .then_inc(restarted, 1)
                            dve.wait_ge(restarted, p + ph.before + 1)
                        return end

                    def restore_first():
                        for ht, part in ((ht_hi, first_hi), (ht_lo, first_lo)):
                            dve.tensor_copy(ht[:, :, :].rearrange("p k (b c) -> p b k c", b=B)[:, :, :, 0],
                                            part[:, :, :].bitcast(F32)).then_inc(first_split, 1)

                    dve.tensor_copy(first_hi[:], c_cols[:]).then_inc(first_split, 1)
                    dve.wait_ge(first_split, 1)
                    dve.tensor_tensor(first_lo[:], c_cols[:], first_hi[:, :, :].bitcast(F32),
                                      ALU.subtract).then_inc(first_split, 1)
                    dve.wait_ge(first_split, 2)
                    dve.wait_ge(cleared, 5)
                    restore_first()
                    dve.wait_ge(first_split, 4)
                    for ph in (low, full, rest):
                        dve.sem_inc(ph.gates_ready, 8)
                        dve.sem_inc(ph.y_ready, 1)
                        for j in range(2):
                            dve.sem_inc(ph.y_out[j], 16)

                    def start(ph):
                        for ready in (ph.h_ready, ph.ht_hi_ready, ph.ht_lo_ready):
                            dve.sem_inc(ready, 4)

                    start(low)
                    run(dve, low, step, restart(lambda p: bass.ds(p, 1)))
                    start(full)
                    run(dve, full, step, restart(lambda p: bass.ds(p, 1)))

                    for n, state in enumerate((h_end, c_start)):
                        dve.tensor_tensor(pre[:, n, :, :].rearrange("p g j -> p (g j)"), state[:, 1, :],
                                          state[:, 0, :], ALU.subtract).then_inc(moved, 1)
                        dve.wait_ge(moved, 2 * n + 1)
                        dif = pre[:, n, :, :].rearrange("p g j -> p (g j)")
                        dve.tensor_tensor_reduce(gates[:, n, :, :].rearrange("p g j -> p (g j)"), dif, dif, 1.0, 0.0,
                                                 ALU.mult, ALU.max, moved_sq[:, n:n + 1]).then_inc(moved, 1)
                    dve.wait_ge(moved, 4)
                    dve.tensor_reduce(moved_max[:], moved_sq[:], AX.X, ALU.max).then_inc(moved, 1)
                    dve.wait_ge(moved, 5)
                    dve.tensor_scalar(settled[:], moved_max[:], STATE_TOL * STATE_TOL, None,
                                      ALU.is_le).then_inc(settled_ready, 1)
                    dve.wait_ge(settled_summed, 1)
                    dve.tensor_copy(settled_rows[:], settled_sum).then_inc(flag_ready, 1)
                    with unsettled(dve):
                        start(rest)
                        run(dve, rest, step, restart(lambda p: slice(0, 1)))

                @block.tensor
                def _(pe):
                    pe.wait_ge(wh_ready, HB)

                    def turn(ph, p, k, first):
                        pe.wait_ge(ph.h_ready, first + 4 * p + k + 1)
                        pe.transpose(h_turn[k], h[:, k, :], ident[:]).then_inc(ph.h_turned, 1)

                    def step(ph, p, n, s, j):
                        first = 8 * n + 4 * j

                        def fill(b):
                            if b not in ph.by_pe:
                                return
                            if b == ph.by_pe[0]:
                                pe.wait_ge(ph.xz_in[j], 16 * n + 16)
                            pe.wait_ge(ph.gates_ready, first + b + 5)
                            pe.matmul(z[:, b, :], ident[:], xz[:, j, b, :, :].rearrange("p g j -> p (g j)"),
                                      start=True, stop=False)

                        def add(k, b, parts):
                            if k == 0 and parts[0] == 0 and b not in ph.by_pe:
                                pe.wait_ge(ph.gates_ready, first + b + 5)
                            hi = w_hi[:, k, :].rearrange("p (g b j) -> p b g j", g=4, b=HB)[:, b]
                            lo = w_lo[:, k, :].rearrange("p (g b j) -> p b g j", g=4, b=HB)[:, b]
                            pairs = [(ht_hi, hi), (ht_hi, lo), (ht_lo, hi)] if ph.full else [(ht_hi, hi)]
                            for i in parts:
                                starts = k == 0 and i == 0 and b not in ph.by_pe
                                ends = k == HB - 1 and i == len(pairs) - 1
                                last = pe.matmul(z[:, b, :], pairs[i][0][:, k, :], pairs[i][1], start=starts, stop=ends)
                                if ends:
                                    last.then_inc(ph.summed, 1)

                        def hi_taken(k):
                            pe.wait_ge(ph.ht_hi_ready, first + 4 * p + k + 1)

                        def lo_taken(k):
                            if ph.full:
                                pe.wait_ge(ph.ht_lo_ready, first + 4 * p + k + 1)

                        every = [0, 1, 2] if ph.full else [0]
                        if ph.full:
                            turn(ph, p, 0, first)
                            turn(ph, p, 1, first)
                            hi_taken(0)
                            for b in range(HB):
                                add(0, b, [0, 1])
                            lo_taken(0)
                            for b in range(HB):
                                add(0, b, [2])
                            turn(ph, p, 2, first)
                            hi_taken(1)
                            lo_taken(1)
                            for b in range(HB):
                                if b == 2:
                                    turn(ph, p, 3, first)
                                add(1, b, every)
                        else:
                            fill(0)
                            fill(1)
                            turn(ph, p, 0, first)
                            fill(2)
                            turn(ph, p, 1, first)
                            fill(3)
                            turn(ph, p, 2, first)
                            hi_taken(0)
                            for b in range(HB):
                                add(0, b, every)
                            turn(ph, p, 3, first)
                            hi_taken(1)
                            for b in range(HB):
                                add(1, b, every)
                        hi_taken(HB - 1)
                        lo_taken(HB - 1)
                        for b in range(HB):
                            for k in range(2, HB):
                                add(k, b, every)

                    def end(ph, p):
                        for k in range(HB):
                            turn(ph, p, k, 4 * L * p + 4 * L)

                    run(pe, low, step, end)
                    run(pe, full, step, end)
                    pe.wait_ge(settled_ready, 1)
                    pe.matmul(settled_sum, settled[:], ones[:, 0:1], start=True, stop=True).then_inc(settled_summed, 1)
                    with unsettled(pe):
                        run(pe, rest, step, end)


_INS = ['x', 'fside_BxS_0', 'cond_1024', 'L1_cond_Wx', 'L1_cond_Wh', 'L1_cond_b']
_OUTS = [((2, 2048, 512), 'float32')]


def kernel(**inputs):
    import numpy as _np
    import concourse.bacc as _bacc
    from concourse import mybir as _mybir
    from concourse.bass_utils import run_bass_kernel_spmd as _run

    nc = _bacc.Bacc("TRN2", target_bir_lowering=False, num_devices=1)
    arrays, args = {}, []
    for name in _INS:
        a = _np.ascontiguousarray(inputs[name])
        arrays[f"in_{name}_dram"] = a
        args.append(nc.dram_tensor(f"in_{name}_dram", a.shape, _mybir.dt.from_np(a.dtype), kind="ExternalInput").ap())
    for i, (shape, dtype) in enumerate(_OUTS):
        dt = _mybir.dt.from_np(_np.dtype(dtype))
        args.append(nc.dram_tensor(f"out_{i}_dram", shape, dt, kind="ExternalOutput").ap())
    sinkhorn_lstm(nc, *args)
    r = _run(nc, [arrays], core_ids=[0])
    return r.results[0]["out_0_dram"]
```

```python
from contextlib import ExitStack

import concourse.bass as bass
import numpy as np
from concourse import mybir

ALU = mybir.AluOpType
ACT = mybir.ActivationFunctionType
AX = mybir.AxisListType
F32 = mybir.dt.float32
F32R = mybir.dt.float32r
I32 = mybir.dt.int32

MU = 0.1
TOL = 1e-09
ITERS = 30
EPS = 1e-12
INV_EPS = float(np.float32(1) / np.float32(EPS))
STATE_TOL = 2.0 ** -18


def sinkhorn_lstm(nc: bass.Bass, x: bass.AP, r: bass.AP, c: bass.AP, wx: bass.AP, wh: bass.AP, bias: bass.AP,
                  out: bass.AP):
    B, N, M = x.shape
    P = 128
    CH = P // B
    L = N // CH
    KC = M // P
    H = wh.shape[0]
    G4 = wh.shape[1]
    HB = H // P
    GROUPS = [(0, 4, 0), (4, 9, 2), (9, 13, 2), (13, 17, 1), (17, 21, 2), (21, 24, 1), (24, 28, 2), (28, 30, 1),
              (30, 32, 1)]
    NG = len(GROUPS)
    OFF = sum(n for _, _, n in GROUPS)
    OWN = L - OFF
    LC = 4
    NLC = L // LC
    LO_BY_POOL = [2, 5]
    LOW, FULL, REST = 1, 2, CH - 2
    SKIP = L // 4
    assert B * CH == P and H == M and G4 == 4 * H and L % 2 == 0

    x_v = x.rearrange("b (c s) m -> (b c) s m", c=CH)
    out_v = out.rearrange("b (c s) m -> (b c) s m", c=CH)
    r_v = r.rearrange("b (c s) -> (b c) s", c=CH)
    c_v = c.rearrange("b (k j) -> (b k) j", j=P)
    wx_v = wx.rearrange("(k p) n -> k p n", p=P)
    wh_v = wh.rearrange("(k p) n -> k p n", p=P)
    xz_dram = nc.dram_tensor("xz_scratch", [L, P, G4], F32, kind="Internal").ap()

    ctx = ExitStack()
    with ctx:
        def sb(name, shape, dt, stack=ctx):
            return stack.enter_context(nc.sbuf_tensor(name, shape, dt))

        def pb(name, shape, dt=F32):
            return ctx.enter_context(nc.psum_tensor(name, shape, dt))

        def sem(name):
            return ctx.enter_context(nc.semaphore(name))

        kx = sb("kx", [P, L, M], F32)
        ident = sb("ident", [P, P], F32)
        batch_ones = sb("batch_ones", [P, P], F32)
        ones = sb("ones", [P, P], F32)
        u_row = sb("u_row", [P, L], F32)
        c_cols = sb("c_cols", [P, B, KC], F32)
        v_row = sb("v_row", [P, M], F32)

        z = pb("z", [P, 4, 512])
        p_a = pb("p_a", [P, 512])
        p_b = pb("p_b", [P, 512])
        p_s = pb("p_s", [P, 512])
        p_v = pb("p_v", [P, 512])

        with ExitStack() as mem:
            k_hi = sb("k_hi", [P, L, M], F32R, mem)
            k_lo = sb("k_lo", [P, L, M], F32R, mem)
            r_in = sb("r_in", [P, L], F32, mem)
            c_in = sb("c_in", [B * KC, P], F32, mem)
            exp_sum = sb("exp_sum", [P, NLC], F32, mem)
            one_sum = sb("one_sum", [P, 2], F32, mem)
            inv_sum = sb("inv_sum", [P, 1], F32, mem)
            W0 = 64
            r_cols = sb("r_cols", [P, L, B], F32, mem)
            u = [sb(f"u{n}", [P, L, B], F32, mem) for n in range(2)]
            u_dif = sb("u_dif", [P, L, B], F32, mem)
            u_dif_sq = sb("u_dif_sq", [P, L, B], F32, mem)
            u_parts_all = sb("u_parts", [P, W0 + L * 2 * B], F32R, mem)
            u_parts = u_parts_all[:, W0:].rearrange("p (l h b) -> p l h b", h=2, b=B)
            dif_sq = sb("dif_sq", [P, B], F32, mem)
            dif_max = sb("dif_max", [P, 1], F32, mem)
            active = sb("active", [P, 2], F32, mem)
            c_act = sb("c_act", [P, B, KC], F32, mem)
            v = sb("v", [P, B, KC], F32, mem)
            v_kept = sb("v_kept", [P, B, KC], F32, mem)
            v_new = sb("v_new", [P, B, KC], F32, mem)
            v_wide = sb("v_wide", [P, KC, B, CH], F32, mem)
            w_rows_all = sb("w_rows", [P, M], F32, mem)
            pair_sum_all = sb("pair_sum", [P, B], F32, mem)
            own = slice(W0, W0 + 2 * B)
            w_rows, pair_sum = w_rows_all[own, :], pair_sum_all[own, :]
            product = [z[:, n, :] for n in range(3)]
            off_product = sb("off_product", [P, 2, M], F32, mem)
            p_v_off = z[:, 3, :]
            kv = sb("kv", [P, L], F32, mem)
            kv_inv = sb("kv_inv", [P, L], F32, mem)
            w_inv = sb("w_inv", [P, B, KC], F32, mem)

            p_w, p_small = p_a, p_s
            w_cols = p_small[:, 0:B * KC].rearrange("p (b k) -> p b k", b=B)
            dif_all = p_b[:, 0:B]
            sum_all = p_b[:, 16:17]
            c_turned = p_small[:, 64:64 + B * KC]

            small_in = sem("small_in")
            x_in = [sem(f"x_in{n}") for n in range(NLC)]
            zeroed = sem("zeroed")
            ident_ready = sem("ident_ready")
            exp_ready = sem("exp_ready")
            summed = sem("summed")
            totalled = sem("totalled")
            inv_ready = sem("inv_ready")
            k_ready = sem("k_ready")
            k_hi_ready = sem("k_hi_ready")
            k_lo_ready = [sem(f"k_lo_ready{n}") for n in range(NLC)]
            c_turned_ready = sem("c_turned_ready")
            prepared = sem("prepared")
            parts_hi = sem("parts_hi")
            parts_ready = sem("parts_ready")
            w_ready = sem("w_ready")
            w_copied = sem("w_copied")
            w_cols_ready = sem("w_cols_ready")
            dif_ready = sem("dif_ready")
            dif_squared = sem("dif_squared")
            dif_summed = sem("dif_summed")
            dif_maxed = sem("dif_maxed")
            active_ready = sem("active_ready")
            kept_ready = sem("kept_ready")
            v_new_ready = sem("v_new_ready")
            v_ready = sem("v_ready")
            v_wide_ready = sem("v_wide_ready")
            v_spread = sem("v_spread")
            v_spread_off = sem("v_spread_off")
            v_copied = sem("v_copied")
            off_ready = sem("off_ready")
            off_summed = sem("off_summed")
            kv_ready = sem("kv_ready")
            w_inv_ready = sem("w_inv_ready")
            kv_inv_ready = sem("kv_inv_ready")
            u_ready = sem("u_ready")

            def flat(t):
                return t[:, :, :].rearrange("p l b -> p (l b)")

            with nc.Block() as block:
                @block.sync
                def _(sp):
                    sp.dma_start(r_in[:], r_v).then_inc(small_in, 16)
                    sp.dma_start(c_in[:], c_v).then_inc(small_in, 16)
                    for n in range(NLC):
                        sp.dma_start(kx[:, n * LC:(n + 1) * LC, :], x_v[:, n * LC:(n + 1) * LC, :]).then_inc(x_in[n], 16)

                @block.gpsimd
                def _(pool):
                    pool.memset(ident[:], 0.0).then_inc(zeroed, 1)
                    pool.wait_ge(zeroed, 1)
                    pool.affine_select(out=ident[:], in_=ident[:], compare_op=ALU.not_equal, fill=1.0, base=0,
                                       pattern=[[-1, P]], channel_multiplier=1).then_inc(ident_ready, 1)

                    def iteration(it):
                        pool.wait_ge(v_copied, it + 1)
                        n = 0
                        for _, b, off in GROUPS:
                            for s in range(b - off, b):
                                pool.wait_ge(off_summed, OFF * it + n + 1)
                                pool.tensor_tensor(off_product[:, n % 2, :], kx[:, s, :], v_row[:],
                                                   ALU.mult).then_inc(off_ready, 1)
                                n += 1

                    for n in LO_BY_POOL:
                        sl = slice(n * LC, (n + 1) * LC)
                        pool.wait_ge(k_hi_ready, n + 1)
                        pool.tensor_tensor(k_lo[:, sl, :], kx[:, sl, :], k_hi[:, sl, :].bitcast(F32),
                                           ALU.subtract).then_inc(k_lo_ready[n], 1)
                    pool.sem_inc(off_summed, 2)
                    pool.wait_ge(k_ready, NLC)
                    iteration(0)
                    with pool.Fori(0, ITERS) as it:
                        iteration(it + 1)

                @block.scalar
                def _(act):
                    for n in range(NLC):
                        act.wait_ge(x_in[n], 16)
                        k = kx[:, n * LC:(n + 1) * LC, :]
                        nc.scalar.activation(k, k, ACT.Exp, scale=-1.0 / MU,
                                             accum_out=exp_sum[:, n:n + 1]).then_inc(exp_ready, 1)
                    for n in range(NLC):
                        act.wait_ge(k_ready, n + 1)
                        nc.scalar.copy(k_hi[:, n * LC:(n + 1) * LC, :],
                                       kx[:, n * LC:(n + 1) * LC, :]).then_inc(k_hi_ready, 1)

                    def iteration(it):
                        act.wait_ge(w_ready, it + 1)
                        nc.scalar.copy(w_rows, p_w[own, :]).then_inc(w_copied, 1)
                        act.wait_ge(v_spread_off, it + 1)
                        nc.scalar.copy(v_row[:], p_v_off).then_inc(v_copied, 1)
                        n = 0
                        for _, b, off in GROUPS:
                            for s in range(b - off, b):
                                act.wait_ge(off_ready, OFF * it + n + 1)
                                nc.scalar.activation(off_product[:, n % 2, :], off_product[:, n % 2, :], ACT.Copy,
                                                     accum_out=kv[:, s:s + 1]).then_inc(off_summed, 1)
                                n += 1

                    iteration(0)
                    with act.Fori(0, ITERS) as it:
                        iteration(it + 1)

                @block.vector
                def _(dve):
                    dve.memset(batch_ones[:], 0.0).then_inc(prepared, 1)
                    dve.memset(flat(r_cols), 0.0).then_inc(prepared, 1)
                    dve.memset(flat(u[1]), 0.0).then_inc(prepared, 1)
                    dve.memset(v[:], 0.0).then_inc(prepared, 1)
                    dve.memset(active[:, 1:2], 1.0).then_inc(prepared, 1)
                    dve.memset(ones[:], 1.0).then_inc(prepared, 1)
                    dve.memset(u_parts_all[:, 0:W0].bitcast(F32), 0.0).then_inc(prepared, 1)
                    dve.wait_ge(prepared, 7)
                    dve.wait_ge(small_in, 32)
                    for b in range(B):
                        rows = slice(b * CH, (b + 1) * CH)
                        dve.memset(batch_ones[rows, rows], 1.0).then_inc(prepared, 1)
                        dve.memset(u[1][rows, :, b], 1.0).then_inc(prepared, 1)
                        dve.tensor_copy(r_cols[rows, :, b], r_in[rows, :]).then_inc(prepared, 1)
                    dve.wait_ge(ident_ready, 1)
                    dve.tensor_tensor(pair_sum, ident[own, W0:W0 + B], ident[own, W0 + B:W0 + 2 * B],
                                      ALU.add).then_inc(prepared, 1)
                    dve.wait_ge(prepared, 7 + 3 * B + 1)
                    dve.tensor_copy(flat(u[0]), flat(r_cols)).then_inc(prepared, 1)
                    dve.wait_ge(c_turned_ready, 1)
                    dve.tensor_copy(c_cols[:, :, :].rearrange("p b k -> p (b k)"), c_turned).then_inc(prepared, 1)
                    dve.wait_ge(prepared, 7 + 3 * B + 3)

                    def split_u(un, a, b):
                        dve.tensor_copy(u_parts[:, a:b, 0, :], un[:, a:b, :]).then_inc(parts_hi, 1)

                    def split_lo(un, a, b):
                        dve.tensor_tensor(u_parts[:, a:b, 1, :], un[:, a:b, :], u_parts[:, a:b, 0, :].bitcast(F32),
                                          ALU.subtract).then_inc(parts_ready, 1)

                    for g, (a, b, off) in enumerate(GROUPS):
                        split_u(u[0], a, b)
                        dve.wait_ge(parts_hi, g + 1)
                        split_lo(u[0], a, b)

                    dve.wait_ge(exp_ready, NLC)
                    dve.tensor_reduce(one_sum[:, 0:1], exp_sum[:], AX.X, ALU.add).then_inc(summed, 1)
                    dve.wait_ge(totalled, 1)
                    dve.tensor_scalar(one_sum[:, 1:2], sum_all, EPS, None, ALU.max).then_inc(inv_ready, 1)
                    dve.wait_ge(inv_ready, 1)
                    dve.reciprocal(inv_sum[:], one_sum[:, 1:2]).then_inc(inv_ready, 1)
                    dve.wait_ge(inv_ready, 2)

                    def scale_k(n):
                        k = kx[:, n * LC:(n + 1) * LC, :]
                        dve.tensor_scalar(k, k, inv_sum[:, 0:1], None, ALU.mult).then_inc(k_ready, 1)

                    scale_k(0)
                    scale_k(1)
                    for n in range(NLC):
                        if n + 2 < NLC:
                            scale_k(n + 2)
                        sl = slice(n * LC, (n + 1) * LC)
                        if n not in LO_BY_POOL:
                            dve.wait_ge(k_hi_ready, n + 1)
                            dve.tensor_tensor(k_lo[:, sl, :], kx[:, sl, :], k_hi[:, sl, :].bitcast(F32),
                                              ALU.subtract).then_inc(k_lo_ready[n], 1)

                    def form_u(it, up, g, part):
                        a, b, off = GROUPS[g]
                        inv = kv_inv[:, a:b].unsqueeze(2).to_broadcast([P, b - a, B])
                        if part == 0:
                            dve.wait_ge(kv_ready, OWN * it + sum(e - d - o for d, e, o in GROUPS[:g + 1]))
                            dve.wait_ge(off_summed, OFF * it + sum(o for _, _, o in GROUPS[:g + 1]) + 2)
                            dve.reciprocal(kv_inv[:, a:b], kv[:, a:b]).then_inc(kv_inv_ready, 1)
                        elif part == 1:
                            dve.wait_ge(kv_inv_ready, NG * it + g + 1)
                            dve.scalar_tensor_tensor(out=up[:, a:b, :], in0=inv, scalar=INV_EPS, in1=r_cols[:, a:b, :],
                                                     op0=ALU.min, op1=ALU.mult).then_inc(u_ready, 1)
                            dve.scalar_tensor_tensor(out=u_parts[:, a:b, 0, :], in0=inv, scalar=INV_EPS,
                                                     in1=r_cols[:, a:b, :], op0=ALU.min,
                                                     op1=ALU.mult).then_inc(parts_hi, 1)
                        else:
                            dve.wait_ge(u_ready, NG * it + g + 1)
                            dve.wait_ge(parts_hi, NG * (it + 1) + g + 1)
                            split_lo(up, a, b)

                    def iteration(it, cur):
                        un, up = u[cur], u[1 - cur]
                        dve.tensor_tensor(flat(u_dif), flat(un), flat(up), ALU.subtract).then_inc(dif_ready, 1)
                        dve.wait_ge(dif_ready, it + 1)
                        for b in range(B):
                            dve.tensor_tensor_reduce(u_dif_sq[:, :, b], u_dif[:, :, b], u_dif[:, :, b], 1.0, 0.0,
                                                     ALU.mult, ALU.add, dif_sq[:, b:b + 1]).then_inc(dif_squared, 1)
                        dve.wait_ge(dif_summed, it + 1)
                        dve.tensor_reduce(dif_max[:], dif_all, AX.X, ALU.max).then_inc(dif_maxed, 1)
                        dve.wait_ge(dif_maxed, it + 1)
                        now, before = active[:, cur:cur + 1], active[:, 1 - cur:2 - cur]
                        dve.tensor_scalar(now, dif_max[:], TOL * TOL, before, ALU.is_gt, ALU.min).then_inc(active_ready, 1)
                        dve.wait_ge(active_ready, it + 1)
                        dve.tensor_scalar(c_act[:], c_cols[:], now, None, ALU.mult).then_inc(kept_ready, 1)
                        dve.scalar_tensor_tensor(out=v_kept[:], in0=v[:], scalar=now, in1=v[:], op0=ALU.mult,
                                                 op1=ALU.subtract).then_inc(kept_ready, 1)
                        dve.wait_ge(w_cols_ready, it + 1)
                        dve.reciprocal(w_inv[:], w_cols).then_inc(w_inv_ready, 1)
                        dve.wait_ge(w_inv_ready, it + 1)
                        dve.wait_ge(kept_ready, 2 * it + 2)
                        dve.scalar_tensor_tensor(out=v_new[:], in0=w_inv[:], scalar=INV_EPS, in1=c_act[:], op0=ALU.min,
                                                 op1=ALU.mult).then_inc(v_new_ready, 1)
                        dve.wait_ge(v_new_ready, it + 1)

                        def spread(t, ks):
                            return t[:, :, ks].rearrange("p b k -> p k b").unsqueeze(3).to_broadcast([P, KC // 2, B, CH])

                        for f in range(2):
                            ks = slice(f * KC // 2, (f + 1) * KC // 2)
                            dve.tensor_tensor(v_wide[:, ks, :, :], spread(v_new, ks), spread(v_kept, ks),
                                              ALU.subtract).then_inc(v_wide_ready, 1)
                        dve.tensor_tensor(v[:], v_new[:], v_kept[:], ALU.subtract).then_inc(v_ready, 1)
                        dve.wait_ge(v_spread, it + 1)
                        n = 0
                        for g, (a, b, off) in enumerate(GROUPS):
                            for s in range(a, b - off):
                                if n >= len(product):
                                    dve.wait_ge(kv_ready, OWN * it + n + 1 - len(product))
                                dve.tensor_tensor_reduce(product[n % len(product)], kx[:, s, :], p_v[:], 1.0, 0.0,
                                                         ALU.mult, ALU.add, kv[:, s:s + 1]).then_inc(kv_ready, 1)
                                n += 1
                                if g > 0 and s - a < 3:
                                    form_u(it, up, g - 1, s - a)
                            for part in range(b - off - a, 3):
                                if g > 0:
                                    form_u(it, up, g - 1, part)
                        for part in range(3):
                            form_u(it, up, NG - 1, part)

                    iteration(0, 0)
                    with dve.Fori(0, ITERS // 2) as i:
                        iteration(2 * i + 1, 1)
                        iteration(2 * i + 2, 0)
                    dve.tensor_tensor(u_row[:], u[1][:, :, 0], u[1][:, :, 1], ALU.add)

                @block.tensor
                def _(pe):
                    pe.wait_ge(ident_ready, 1)
                    pe.wait_ge(small_in, 32)
                    pe.transpose(c_turned, c_in[:], ident[0:B * KC, 0:B * KC]).then_inc(c_turned_ready, 1)
                    pe.wait_ge(prepared, 7 + 3 * B + 3)
                    pe.wait_ge(summed, 1)
                    pe.matmul(sum_all, batch_ones[:], one_sum[:, 0:1], start=True, stop=True).then_inc(totalled, 1)

                    def keep_warm(bank, count):
                        for _ in range(count):
                            pe.matmul(bank[:, :], k_hi[:, 0, 0:P], k_hi[:, 0, :], start=True, stop=True)

                    def iteration(it, first=False):
                        for g, (a, b, off) in enumerate(GROUPS):
                            pe.wait_ge(parts_ready, NG * it + g + 1)
                            for s in range(a, b):
                                if first and s % LC == 0:
                                    pe.wait_ge(k_lo_ready[s // LC], 1)
                                parts = u_parts_all[:, s * 2 * B:W0 + (s + 1) * 2 * B]
                                pe.matmul(p_w[0:W0 + 2 * B, :], parts, k_hi[:, s, :], start=(s == 0), stop=False)
                                last = pe.matmul(p_w[0:W0 + 2 * B, :], parts, k_lo[:, s, :], start=False,
                                                 stop=(s == L - 1))
                        last.then_inc(w_ready, 1)
                        pe.wait_ge(dif_squared, B * it + B)
                        pe.matmul(dif_all, ones[:], dif_sq[:], start=True, stop=True).then_inc(dif_summed, 1)
                        pe.wait_ge(w_copied, it + 1)
                        for k in range(KC):
                            last = pe.matmul(w_cols[:, :, k], w_rows[:, k * P:(k + 1) * P], pair_sum,
                                             start=True, stop=True)
                        last.then_inc(w_cols_ready, 1)
                        keep_warm(p_v, 6)
                        for k in range(KC):
                            if k % (KC // 2) == 0:
                                pe.wait_ge(v_wide_ready, 2 * it + 1 + k // (KC // 2))
                            last = pe.transpose(p_v[:, k * P:(k + 1) * P],
                                                v_wide[:, k, :, :].rearrange("p b c -> p (b c)"), ident[:])
                        last.then_inc(v_spread, 1)
                        for k in range(KC):
                            last = pe.transpose(p_v_off[:, k * P:(k + 1) * P],
                                                v_wide[:, k, :, :].rearrange("p b c -> p (b c)"), ident[:])
                        last.then_inc(v_spread_off, 1)
                        keep_warm(p_b, 12)

                    iteration(0, first=True)
                    with pe.Fori(0, ITERS) as it:
                        iteration(it + 1)

        h = sb("h", [P, HB, P], F32)
        cell = sb("cell", [P, HB, P], F32)
        ht_hi = sb("ht_hi", [P, HB, P], F32R)
        wh_hi = sb("wh_hi", [P, HB, G4], F32R)

        with ExitStack() as mem:
            wx_hi = sb("wx_hi", [P, KC, G4], F32R, mem)
            wx_lo = sb("wx_lo", [P, KC, G4], F32R, mem)
            bias_row = sb("bias_row", [P, HB, 4, P], F32, mem)
            x_step = sb("x_step", [P, 2, M], F32, mem)
            xt_hi = sb("xt_hi", [P, 2, KC, P], F32R, mem)
            xt_lo = sb("xt_lo", [P, 2, KC, P], F32R, mem)
            xz = sb("xz_out", [P, HB, 4, P], F32, mem)
            gates = sb("gates_first", [P, HB, 4, P], F32, mem)
            gate_i, gate_f, gate_o, gate_g = [gates[:, :, g, :] for g in range(4)]
            places = [t[:, :, :, :].rearrange("p b g j -> p (b g j)") for t in (xz, gates, bias_row)]
            x_turn = p_a[:, :].rearrange("p (k j) -> p k j", k=KC)
            h_turn = p_b[:, :].rearrange("p (k j) -> p k j", k=HB)

            wx_in = [sem(f"wx_in{k}") for k in range(KC)]
            wh_in = [sem(f"wh_in{k}") for k in range(HB)]
            wx_hi_ready = sem("wx_hi_ready")
            wx_ready = sem("wx_ready")
            wh_rounded = sem("wh_rounded")
            bias_in = sem("bias_in")
            cleared = sem("first_cleared")
            x_step_in = [sem(f"x_step_in{j}") for j in range(2)]
            p_ready = sem("p_ready")
            x1_ready = sem("x1_ready")
            x1_kept = sem("x1_kept")
            x_turned = sem("x_turned")
            xt_hi_ready = sem("xt_hi_ready")
            xt_ready = sem("xt_ready")
            xz_summed = sem("xz_summed")
            xz_taken = sem("xz_taken")
            xz_out = [sem(f"xz_stored{f}") for f in range(2)]
            z_summed = sem("z_summed")
            z_taken = sem("z_taken")
            gates_open = sem("gates_open")
            f_c_ready = sem("f_c_ready")
            i_g_ready = sem("i_g_ready")
            c_ready = sem("c_ready")
            tanh_c_ready = sem("tanh_c_ready")
            h_formed = sem("h_formed")
            h_in_bank = sem("h_in_bank")
            ht_ready = sem("ht_ready")

            def gate_columns(w, k, b):
                return w[:, k, :].rearrange("p (g b j) -> p b g j", g=4, b=HB)[:, b]

            with nc.Block() as block:
                @block.sync
                def _(sp):
                    for f in range(2):
                        sp.sem_inc(xz_out[f], 16)

                    def load(s, j):
                        sp.dma_start(x_step[:, j, :], x_v[:, bass.ds(s, 1), :]).then_inc(x_step_in[j], 16)

                    def store(s):
                        for f in range(2):
                            blocks = slice(f * HB // 2, (f + 1) * HB // 2)
                            sp.wait_ge(xz_taken, 4 * s + 2 * f + 6)
                            columns = slice(f * G4 // 2, (f + 1) * G4 // 2)
                            sp.dma_start(xz_dram[bass.ds(s, 1), :, columns].rearrange("s p n -> p (s n)"),
                                         xz[:, blocks, :, :].rearrange("p b g j -> p (b g j)")).then_inc(xz_out[f], 16)

                    sp.dma_start(places[0], wx_v[0]).then_inc(wx_in[0], 16)
                    load(0, 0)
                    sp.dma_start(places[1], wx_v[1]).then_inc(wx_in[1], 16)
                    sp.dma_start(places[2], wx_v[2]).then_inc(wx_in[2], 16)
                    sp.wait_ge(wx_ready, 1)
                    sp.dma_start(places[0], wx_v[3]).then_inc(wx_in[3], 16)
                    load(1, 1)
                    sp.wait_ge(wx_ready, 3)
                    for g in range(4):
                        sp.dma_start(bias_row[:, :, g, :], bias[g * H:(g + 1) * H].rearrange("(b j) -> b j", b=HB)
                                     .partition_broadcast(P)).then_inc(bias_in, 16)

                    def step(s, j):
                        sp.wait_ge(x1_kept, s + 1)
                        sp.wait_ge(x_turned, s + 1)
                        load(s + 2, j)
                        store(s)

                    for k in range(HB):
                        if k > 0:
                            sp.wait_ge(wh_rounded, k)
                        sp.dma_start(places[1], wh_v[k]).then_inc(wh_in[k], 16)
                        step(k, k % 2)
                    with sp.Fori(0, (L - HB) // 2 - 1) as i:
                        for j in range(2):
                            step(2 * i + j + HB, j)
                    for s in range(L - 2, L):
                        store(s)
                    for f in range(2):
                        sp.wait_ge(xz_out[f], 16 * (L + 1))

                @block.gpsimd
                def _(pool):
                    with pool.Fori(0, L // 2) as i:
                        for j in range(2):
                            s = 2 * i + j
                            pool.wait_ge(p_ready, s + 1)
                            pool.wait_ge(x_step_in[j], 16 * i + 16)
                            pool.tensor_tensor(x_step[:, j:j + 1, :], x_step[:, j:j + 1, :], kx[:, bass.ds(s, 1), :],
                                               ALU.add).then_inc(x1_ready, 1)

                @block.scalar
                def _(act):
                    def keep_x1(s, j):
                        act.wait_ge(x1_ready, s + 1)
                        nc.scalar.copy(kx[:, bass.ds(s, 1), :], x_step[:, j:j + 1, :]).then_inc(x1_kept, 1)

                    def take_xt_hi(s, j):
                        act.wait_ge(x_turned, s + 1)
                        nc.scalar.copy(xt_hi[:, j, :, :], x_turn).then_inc(xt_hi_ready, 1)

                    def take_ht(n):
                        act.wait_ge(h_in_bank, n + 1)
                        nc.scalar.copy(ht_hi[:], h_turn).then_inc(ht_ready, 1)

                    def open_gates(n):
                        for b in range(HB):
                            act.wait_ge(z_taken, 4 * n + b + 5)
                            nc.scalar.activation(gates[:, b, 0:3, :], gates[:, b, 0:3, :], ACT.Sigmoid)
                            nc.scalar.activation(gates[:, b, 3, :], gates[:, b, 3, :], ACT.Tanh).then_inc(gates_open, 1)
                        act.wait_ge(c_ready, n + 1)
                        nc.scalar.activation(gate_g, cell[:], ACT.Tanh).then_inc(tanh_c_ready, 1)

                    for k in range(KC):
                        act.wait_ge(wx_in[k], 16)
                        nc.scalar.copy(wx_hi[:, k, :], places[k % 3]).then_inc(wx_hi_ready, 1)
                        if k == 0:
                            take_xt_hi(0, 0)
                    keep_x1(0, 0)
                    for k in range(HB):
                        keep_x1(k + 1, 1 - k % 2)
                        take_xt_hi(k + 1, 1 - k % 2)
                        act.wait_ge(wh_in[k], 16)
                        nc.scalar.copy(wh_hi[:, k, :], places[1]).then_inc(wh_rounded, 1)
                    with act.Fori(0, (SKIP - HB) // 2) as i:
                        for j in range(2):
                            s = 2 * i + j + HB
                            keep_x1(s + 1, 1 - j)
                            take_xt_hi(s + 1, 1 - j)
                    nc.scalar.preload_act_table_set("sigmoid_and_others")
                    with act.Fori(0, (L - SKIP) // 2 - 1) as i:
                        for j in range(2):
                            n = 2 * i + j
                            take_xt_hi(n + SKIP + 1, 1 - j)
                            take_ht(n)
                            open_gates(n)
                            keep_x1(n + SKIP + 1, 1 - j)
                    n = L - SKIP - 2
                    take_xt_hi(n + SKIP + 1, 1)
                    take_ht(n)
                    open_gates(n)
                    keep_x1(n + SKIP + 1, 1)
                    take_ht(n + 1)
                    open_gates(n + 1)

                @block.vector
                def _(dve):
                    def form_p(s):
                        dve.scalar_tensor_tensor(out=kx[:, bass.ds(s, 1), :], in0=kx[:, bass.ds(s, 1), :],
                                                 scalar=u_row[:, bass.ds(s, 1)], in1=v_row[:, :].unsqueeze(1),
                                                 op0=ALU.mult, op1=ALU.mult).then_inc(p_ready, 1)

                    def split_x(s, j):
                        dve.wait_ge(xt_hi_ready, s + 1)
                        dve.tensor_tensor(xt_lo[:, j, :, :], x_turn, xt_hi[:, j, :, :].bitcast(F32),
                                          ALU.subtract).then_inc(xt_ready, 1)

                    def bank(b):
                        return z[:, b, :].rearrange("p (g j) -> p g j", g=4)

                    def take_xz(s, blocks):
                        for b in blocks:
                            if b % 2 == 0:
                                dve.wait_ge(xz_out[b // 2], 16 * s + 16)
                            dve.wait_ge(xz_summed, 4 * s + b + 1)
                            dve.tensor_tensor(xz[:, b, :, :], bank(b), bias_row[:, b, :, :],
                                              ALU.add).then_inc(xz_taken, 1)

                    def take_z(n):
                        dve.wait_ge(h_formed, n + 1)
                        for b in range(HB):
                            dve.wait_ge(z_summed, 4 * n + b + 1)
                            dve.tensor_tensor(gates[:, b, :, :], bank(b), xz[:, b, :, :], ALU.add).then_inc(z_taken, 1)

                    def advance(n):
                        dve.wait_ge(gates_open, 4 * n + 4)
                        dve.tensor_tensor(gate_f, gate_f, cell[:], ALU.mult).then_inc(f_c_ready, 1)
                        dve.tensor_tensor(gate_i, gate_i, gate_g, ALU.mult).then_inc(i_g_ready, 1)
                        dve.wait_ge(f_c_ready, n + 1)
                        dve.wait_ge(i_g_ready, n + 1)
                        dve.tensor_tensor(cell[:], gate_f, gate_i, ALU.add).then_inc(c_ready, 1)
                        dve.wait_ge(tanh_c_ready, n + 1)
                        dve.wait_ge(h_in_bank, n + 1)
                        dve.tensor_tensor(h[:], gate_o, gate_g, ALU.mult).then_inc(h_formed, 1)

                    dve.memset(cell[:], 0.0).then_inc(cleared, 1)
                    dve.memset(h[:], 0.0).then_inc(h_formed, 1)
                    form_p(0)
                    form_p(1)
                    for k in range(KC):
                        dve.wait_ge(wx_hi_ready, k + 1)
                        dve.tensor_tensor(wx_lo[:, k, :], places[k % 3], wx_hi[:, k, :].bitcast(F32),
                                          ALU.subtract).then_inc(wx_ready, 1)
                        if k == 0:
                            split_x(0, 0)
                    dve.wait_ge(bias_in, 64)
                    dve.wait_ge(cleared, 1)
                    with dve.Fori(0, SKIP // 2) as i:
                        for j in range(2):
                            s = 2 * i + j
                            form_p(s + 2)
                            take_xz(s, range(HB - 1))
                            split_x(s + 1, 1 - j)
                            take_xz(s, [HB - 1])
                    with dve.Fori(0, (L - SKIP) // 2 - 1) as i:
                        for j in range(2):
                            n = 2 * i + j
                            take_xz(n + SKIP, range(HB - 1))
                            split_x(n + SKIP + 1, 1 - j)
                            take_xz(n + SKIP, [HB - 1])
                            take_z(n)
                            form_p(n + SKIP + 2)
                            advance(n)
                    n = L - SKIP - 2
                    take_xz(L - 2, range(HB - 1))
                    split_x(L - 1, 1)
                    take_xz(L - 2, [HB - 1])
                    take_z(n)
                    advance(n)
                    take_xz(L - 1, range(HB))
                    take_z(n + 1)
                    advance(n + 1)

                @block.tensor
                def _(pe):
                    pe.sem_inc(xz_taken, 4)
                    pe.sem_inc(z_taken, 4)

                    def turn_x(s, j):
                        pe.wait_ge(x1_ready, s + 1)
                        for k in range(KC):
                            last = pe.transpose(x_turn[:, k, :], x_step[:, j, k * P:(k + 1) * P], ident[:])
                        last.then_inc(x_turned, 1)

                    def turn_h(n):
                        pe.wait_ge(h_formed, n + 1)
                        for k in range(HB):
                            last = pe.transpose(h_turn[:, k, :], h[:, k, :], ident[:])
                        last.then_inc(h_in_bank, 1)

                    def products(j, k, b):
                        hi, lo = gate_columns(wx_hi, k, b), gate_columns(wx_lo, k, b)
                        pe.matmul(z[:, b, :], xt_hi[:, j, k, :], hi, start=(k == 0), stop=False)
                        pe.matmul(z[:, b, :], xt_hi[:, j, k, :], lo, start=False, stop=False)
                        return pe.matmul(z[:, b, :], xt_lo[:, j, k, :], hi, start=False, stop=(k == KC - 1))

                    def project(s, j, blocks, taken, count):
                        for b in blocks:
                            pe.wait_ge(taken, count + b + 1)
                            for k in range(KC):
                                last = products(j, k, b)
                            last.then_inc(xz_summed, 1)

                    def add_h(n):
                        pe.wait_ge(ht_ready, n + 1)
                        for b in range(HB):
                            pe.wait_ge(xz_taken, 4 * (n + SKIP) + b + 5)
                            for k in range(HB):
                                last = pe.matmul(z[:, b, :], ht_hi[:, k, :], gate_columns(wh_hi, k, b), start=(k == 0),
                                                 stop=(k == HB - 1))
                            last.then_inc(z_summed, 1)

                    turn_x(0, 0)
                    pe.wait_ge(xt_ready, 1)
                    for k in range(KC):
                        if k == KC - 1:
                            turn_x(1, 1)
                        pe.wait_ge(wx_ready, k + 1)
                        for b in range(HB):
                            last = products(0, k, b)
                            if k == KC - 1:
                                last.then_inc(xz_summed, 1)
                    pe.wait_ge(xt_ready, 2)
                    project(1, 1, range(HB - 1), xz_taken, 4)
                    turn_x(2, 0)
                    project(1, 1, [HB - 1], xz_taken, 4)
                    with pe.Fori(0, SKIP // 2 - 1) as i:
                        for j in range(2):
                            s = 2 * i + j + 2
                            pe.wait_ge(xt_ready, s + 1)
                            project(s, j, range(HB - 1), xz_taken, 4 * s)
                            turn_x(s + 1, 1 - j)
                            project(s, j, [HB - 1], xz_taken, 4 * s)
                    pe.wait_ge(xz_taken, 4 * SKIP + 4)
                    pe.wait_ge(wh_rounded, HB)

                    def step(n, j, more):
                        s = n + SKIP
                        pe.wait_ge(xt_ready, s + 1)
                        project(s, j, range(HB - 1), z_taken, 4 * n)
                        if more:
                            turn_x(s + 1, 1 - j)
                        turn_h(n)
                        project(s, j, [HB - 1], z_taken, 4 * n)
                        add_h(n)

                    with pe.Fori(0, (L - SKIP) // 2 - 1) as i:
                        for j in range(2):
                            step(2 * i + j, j, True)
                    step(L - SKIP - 2, 0, True)
                    step(L - SKIP - 1, 1, False)

        with ExitStack() as mem:
            wh_lo = sb("wh_lo", [P, HB, G4], F32R, mem)
            xz = sb("xz_in", [P, 2, HB, 4, P], F32, mem)
            pre = sb("pre", [P, HB, 4, P], F32, mem)
            gates = sb("gates", [P, HB, 4, P], F32, mem)
            kept = sb("kept", [P, HB, P], F32, mem)
            added = sb("added", [P, HB, P], F32, mem)
            squashed = sb("squashed", [P, HB, P], F32, mem)
            ht_lo = sb("ht_lo", [P, HB, P], F32R, mem)
            first_hi = sb("first_hi", [P, B, KC], F32R, mem)
            first_lo = sb("first_lo", [P, B, KC], F32R, mem)
            h_end = sb("h_end", [P, 2, H], F32, mem)
            c_start = sb("c_start", [P, 2, H], F32, mem)
            y = sb("y", [P, 2, H], F32, mem)
            moved_sq = sb("moved_sq", [P, 2], F32, mem)
            moved_max = sb("moved_max", [P, 1], F32, mem)
            settled = sb("settled", [P, 1], F32, mem)
            settled_rows = sb("settled_rows", [1, 1], I32, mem)
            h_turn = [bank[:, 0:P] for bank in (p_a, p_b, p_s, p_v)]
            settled_sum = p_s[0:1, 0:1]

            wh_again = [sem(f"wh_again{k}") for k in range(HB)]
            wh_lo_ready = sem("wh_lo_ready")
            ends_turned = sem("ends_turned")
            ends_taken = sem("ends_taken")
            ends_shifted = sem("ends_shifted")
            cell_started = sem("cell_started")
            cleared = sem("cleared")
            first_split = sem("first_split")
            low_lo_ready = sem("low_lo_ready")
            shifted = sem("shifted")
            restarted = sem("restarted")
            moved = sem("moved")
            settled_ready = sem("settled_ready")
            settled_summed = sem("settled_summed")
            flag_ready = sem("flag_ready")

            class Phase:

                def __init__(self, name, before, count, full):
                    self.before, self.count, self.full = before, count, full
                    self.by_pe = 0 if full else HB // 2
                    self.by_dve = HB - self.by_pe
                    self.xz_in = [sem(f"{name}_xz_in{j}") for j in range(2)]
                    self.h_turned = sem(f"{name}_h_turned")
                    self.ht_hi_ready = sem(f"{name}_ht_hi_ready")
                    self.ht_lo_ready = sem(f"{name}_ht_lo_ready")
                    self.summed = sem(f"{name}_summed")
                    self.pre_ready = sem(f"{name}_pre_ready")
                    self.gates_ready = sem(f"{name}_gates_ready")
                    self.kept_ready = sem(f"{name}_kept_ready")
                    self.added_ready = sem(f"{name}_added_ready")
                    self.cell_ready = sem(f"{name}_cell_ready")
                    self.squashed_ready = sem(f"{name}_squashed_ready")
                    self.h_ready = sem(f"{name}_h_ready")
                    self.ended = sem(f"{name}_ended")
                    self.y_ready = sem(f"{name}_y_ready")
                    self.y_out = [sem(f"{name}_y_stored{j}") for j in range(2)]

            low = Phase("low", 0, LOW, False)
            full = Phase("full", LOW, FULL, True)
            rest = Phase("rest", LOW + FULL, REST, True)

            def run(eng, ph, step, end=None, begin=None):
                with eng.Fori(0, ph.count) as p:
                    if begin:
                        begin(ph, p)
                    with eng.Fori(0, L // 2) as i:
                        for j in range(2):
                            step(ph, p, p * (L // 2) + i, 2 * i + j, j)
                    if end:
                        end(ph, p)

            def later(ht, k):
                return ht[:, k, :].rearrange("p (b c) -> p b c", b=B)[:, :, 1:CH]

            def earlier(k):
                return h_turn[k].rearrange("p (b c) -> p b c", b=B)[:, :, 0:CH - 1]

            def unsettled(eng):
                eng.wait_ge(flag_ready, 1)
                rows = eng.value_load(settled_rows[0:1, 0:1], min_val=0, max_val=P)
                return eng.If(rows < P)

            with nc.Block() as block:
                @block.sync
                def _(sp):
                    sp.wait_ge(cleared, 1)
                    for b in range(B):
                        a = b * CH
                        sp.dma_start(c_start[a + 1:a + CH, 0, :],
                                     cell[a:a + CH - 1, :, :].rearrange("p b j -> p (b j)")).then_inc(ends_shifted, 16)

                    def load(ph, n, s, j):
                        sp.wait_ge(ph.gates_ready, 8 * n + 4 * j + 4)
                        sp.dma_start(xz[:, j, :, :, :].rearrange("p b g j -> p (b g j)"),
                                     xz_dram[bass.ds(s, 1), :, :].rearrange("s p n -> p (s n)")) \
                            .then_inc(ph.xz_in[j], 16)

                    def store(ph, n, s, j):
                        sp.wait_ge(ph.y_ready, 2 * n + j + 2)
                        sp.dma_start(out_v[:, bass.ds(s, 1), :], y[:, j:j + 1, :]).then_inc(ph.y_out[j], 16)

                    def passes(ph, slot_of):
                        with sp.Fori(0, ph.count) as p:
                            first = p * (L // 2)
                            for j in range(2):
                                load(ph, first, j, j)
                            with sp.Fori(0, L // 2 - 1) as i:
                                for j in range(2):
                                    if ph.full:
                                        store(ph, first + i, 2 * i + j, j)
                                    load(ph, first + i + 1, 2 * i + j + 2, j)
                            if ph.full:
                                for j in range(2):
                                    store(ph, first + L // 2 - 1, L - 2 + j, j)
                            sp.wait_ge(ph.h_ready, (4 * L + 4) * p + 4 * L + 4)
                            slot = slot_of(p)
                            for b in range(B):
                                a = b * CH
                                sp.dma_start(c_start[a + 1:a + CH, slot, :],
                                             cell[a:a + CH - 1, :, :].rearrange("p b j -> p (b j)").unsqueeze(1)) \
                                    .then_inc(shifted, 16)
                        if ph.full:
                            for j in range(2):
                                sp.wait_ge(ph.y_out[j], 16 * (ph.count * (L // 2) + 1))

                    passes(low, lambda p: bass.ds(p, 1))
                    passes(full, lambda p: bass.ds(p, 1))
                    with unsettled(sp):
                        passes(rest, lambda p: slice(0, 1))

                @block.gpsimd
                def _(pool):
                    pool.memset(c_start[:], 0.0).then_inc(cleared, 1)
                    pool.wait_ge(low.xz_in[1], 16)
                    place = y[:, :, :].rearrange("p s j -> p (s j)")
                    for k in range(HB):
                        for f in range(2):
                            half = slice(f * 2 * H, (f + 1) * 2 * H)
                            if k + f > 0:
                                pool.wait_ge(wh_lo_ready, 2 * k + f)
                            pool.dma_start(place, wh_v[k][:, half]).then_inc(wh_again[k], 16)
                            pool.wait_ge(wh_again[k], 16 * f + 16)
                            pool.tensor_tensor(wh_lo[:, k, half], place, wh_hi[:, k, half].bitcast(F32),
                                               ALU.subtract).then_inc(wh_lo_ready, 1)

                    def step(ph, p, n, s, j):
                        for b in range(HB):
                            pool.wait_ge(ph.gates_ready, 8 * n + 4 * j + b + 9)
                            pool.tensor_tensor(added[:, b, :], gates[:, b, 0, :], gates[:, b, 3, :],
                                               ALU.mult).then_inc(ph.added_ready, 1)
                        pool.wait_ge(ph.h_ready, 8 * n + 4 * j + 4 * p + 8)
                        pool.wait_ge(ph.y_out[j], 16 * n + 16)
                        pool.tensor_tensor(y[:, j:j + 1, :], kx[:, bass.ds(s, 1), :],
                                           h[:, :, :].rearrange("p b j -> p (b j)").unsqueeze(1),
                                           ALU.add).then_inc(ph.y_ready, 1)

                    run(pool, full, step)
                    with unsettled(pool):
                        run(pool, rest, step)

                @block.scalar
                def _(act):
                    def step(ph, p, n, s, j):
                        first = 8 * n + 4 * j

                        def open_gates(b):
                            if b >= ph.by_pe:
                                act.wait_ge(ph.pre_ready, ph.by_dve * (2 * n + j + 1) + b - ph.by_pe + 1)
                                opened = pre[:, b, :, :]
                            else:
                                act.wait_ge(ph.summed, first + b + 1)
                                opened = z[:, b, :].rearrange("p (g j) -> p g j", g=4)
                            nc.scalar.activation(gates[:, b, 0:3, :], opened[:, 0:3, :], ACT.Sigmoid)
                            nc.scalar.activation(gates[:, b, 3, :], opened[:, 3, :],
                                                 ACT.Tanh).then_inc(ph.gates_ready, 1)

                        def squash(b):
                            act.wait_ge(ph.cell_ready, first + b + 1)
                            nc.scalar.activation(squashed[:, b, :], cell[:, b, :],
                                                 ACT.Tanh).then_inc(ph.squashed_ready, 1)

                        def take_hi(b):
                            act.wait_ge(ph.h_turned, first + 4 * p + b + 5)
                            nc.scalar.copy(ht_hi[:, b, :], h_turn[b]).then_inc(ph.ht_hi_ready, 1)

                        open_gates(0)
                        if ph.full:
                            squash(0)
                            open_gates(1)
                            take_hi(0)
                            open_gates(2)
                            squash(1)
                            open_gates(3)
                            squash(2)
                            take_hi(1)
                            squash(3)
                        else:
                            open_gates(1)
                            open_gates(2)
                            squash(0)
                            squash(1)
                            open_gates(3)
                            take_hi(0)
                            take_hi(1)
                            squash(2)
                            squash(3)
                        take_hi(2)
                        take_hi(3)

                    def end(ph, p):
                        act.wait_ge(ph.ended, p + 1)
                        for k in range(HB):
                            nc.scalar.copy(later(ht_hi, k), earlier(k)).then_inc(ph.ht_hi_ready, 1)

                    for k in range(HB):
                        act.wait_ge(ends_turned, k + 1)
                        nc.scalar.copy(later(ht_hi, k), earlier(k)).then_inc(ends_taken, 1)
                    nc.scalar.preload_act_table_set("sigmoid_and_others")
                    run(act, low, step, end)
                    run(act, full, step, end)
                    with unsettled(act):
                        run(act, rest, step, end)

                @block.vector
                def _(dve):
                    def step(ph, p, n, s, j):
                        first = 8 * n + 4 * j
                        def add_input(b):
                            if b == ph.by_pe:
                                dve.wait_ge(ph.xz_in[j], 16 * n + 16)
                            dve.wait_ge(ph.summed, first + b + 1)
                            dve.tensor_tensor(pre[:, b, :, :], z[:, b, :].rearrange("p (g j) -> p g j", g=4),
                                              xz[:, j, b, :, :], ALU.add).then_inc(ph.pre_ready, 1)

                        def scale_cell(b):
                            dve.wait_ge(ph.gates_ready, first + b + 9)
                            dve.tensor_tensor(kept[:, b, :], gates[:, b, 1, :], cell[:, b, :],
                                              ALU.mult).then_inc(ph.kept_ready, 1)
                            if not ph.full:
                                dve.tensor_tensor(added[:, b, :], gates[:, b, 0, :], gates[:, b, 3, :],
                                                  ALU.mult).then_inc(ph.added_ready, 1)

                        def update_cell(b):
                            dve.wait_ge(ph.kept_ready, first + b + 1)
                            dve.wait_ge(ph.added_ready, first + b + 1)
                            dve.tensor_tensor(cell[:, b, :], kept[:, b, :], added[:, b, :],
                                              ALU.add).then_inc(ph.cell_ready, 1)

                        def form_h(b):
                            dve.wait_ge(ph.squashed_ready, first + b + 1)
                            if ph.full and b == 0:
                                dve.wait_ge(ph.y_ready, 2 * n + j + 1)
                            dve.tensor_tensor(h[:, b, :], gates[:, b, 2, :], squashed[:, b, :],
                                              ALU.mult).then_inc(ph.h_ready, 1)

                        def take_lo(b):
                            if ph.full:
                                dve.wait_ge(ph.ht_hi_ready, first + 4 * p + b + 5)
                                dve.tensor_tensor(ht_lo[:, b, :], h_turn[b], ht_hi[:, b, :].bitcast(F32),
                                                  ALU.subtract).then_inc(ph.ht_lo_ready, 1)

                        if ph.full:
                            add_input(0)
                            scale_cell(0)
                            update_cell(0)
                            add_input(1)
                            form_h(0)
                            add_input(2)
                            scale_cell(1)
                            update_cell(1)
                            add_input(3)
                            form_h(1)
                            take_lo(0)
                            scale_cell(2)
                            update_cell(2)
                            scale_cell(3)
                            update_cell(3)
                            take_lo(1)
                            form_h(2)
                            form_h(3)
                            take_lo(2)
                            take_lo(3)
                        else:
                            scale_cell(0)
                            add_input(2)
                            scale_cell(1)
                            update_cell(0)
                            update_cell(1)
                            add_input(3)
                            form_h(0)
                            form_h(1)
                            scale_cell(2)
                            scale_cell(3)
                            update_cell(2)
                            update_cell(3)
                            form_h(2)
                            form_h(3)

                    def restart(slot_of):
                        def end(ph, p):
                            last = 4 * L + (4 * L + 4) * p
                            if ph.full:
                                dve.wait_ge(ph.ht_lo_ready, last + 4)
                            else:
                                dve.wait_ge(ph.ht_hi_ready, last + 4)
                            dve.wait_ge(ph.h_turned, last + 4)
                            dve.tensor_copy(h_end[:, slot_of(p), :].rearrange("p s j -> p (s j)"),
                                            h[:, :, :].rearrange("p b j -> p (b j)")).then_inc(ph.ended, 1)
                            for b in range(HB):
                                dve.wait_ge(ph.ht_hi_ready, last + b + 5)
                                dve.tensor_tensor(later(ht_lo, b), earlier(b), later(ht_hi, b).bitcast(F32),
                                                  ALU.subtract).then_inc(ph.ht_lo_ready if ph.full else low_lo_ready, 1)
                            restore_first()
                            dve.wait_ge(first_split, 2 + 2 * p + 2 * (ph.before + 2))
                            if ph.full:
                                dve.wait_ge(ph.ht_lo_ready, last + 8)
                            else:
                                dve.wait_ge(low_lo_ready, 4 * p + 4)
                            dve.sem_inc(ph.h_ready, 4)
                            dve.wait_ge(shifted, 16 * B * p + 16 * B * (ph.before + 1))
                            dve.tensor_copy(cell[:, :, :].rearrange("p b j -> p (b j)"),
                                            c_start[:, slot_of(p), :].rearrange("p s j -> p (s j)")) \
                                .then_inc(restarted, 1)
                            dve.wait_ge(restarted, p + ph.before + 1)
                        return end

                    def restore_first():
                        for ht, part in ((ht_hi, first_hi), (ht_lo, first_lo)):
                            dve.tensor_copy(ht[:, :, :].rearrange("p k (b c) -> p b k c", b=B)[:, :, :, 0],
                                            part[:, :, :].bitcast(F32)).then_inc(first_split, 1)

                    for ph in (low, full, rest):
                        dve.sem_inc(ph.pre_ready, ph.by_dve)
                        dve.sem_inc(ph.gates_ready, 8)
                        dve.sem_inc(ph.y_ready, 1)
                        for j in range(2):
                            dve.sem_inc(ph.y_out[j], 16)

                    dve.tensor_copy(first_hi[:], c_cols[:]).then_inc(first_split, 1)
                    dve.wait_ge(first_split, 1)
                    dve.tensor_tensor(first_lo[:], c_cols[:], first_hi[:, :, :].bitcast(F32),
                                      ALU.subtract).then_inc(first_split, 1)
                    dve.wait_ge(first_split, 2)
                    dve.wait_ge(ends_taken, HB)
                    restore_first()
                    dve.wait_ge(first_split, 4)
                    dve.wait_ge(ends_shifted, 16 * B)
                    dve.tensor_copy(cell[:, :, :].rearrange("p b j -> p (b j)"), c_start[:, 0, :]).then_inc(cell_started, 1)
                    dve.wait_ge(cell_started, 1)
                    def start(ph):
                        for ready in (ph.h_ready, ph.ht_hi_ready, ph.ht_lo_ready):
                            dve.sem_inc(ready, 4)

                    start(low)
                    run(dve, low, step, restart(lambda p: bass.ds(p, 1)))
                    start(full)
                    run(dve, full, step, restart(lambda p: bass.ds(p, 1)))

                    for n, state in enumerate((h_end, c_start)):
                        dve.tensor_tensor(pre[:, n, :, :].rearrange("p g j -> p (g j)"), state[:, 1, :],
                                          state[:, 0, :], ALU.subtract).then_inc(moved, 1)
                        dve.wait_ge(moved, 2 * n + 1)
                        dif = pre[:, n, :, :].rearrange("p g j -> p (g j)")
                        dve.tensor_tensor_reduce(gates[:, n, :, :].rearrange("p g j -> p (g j)"), dif, dif, 1.0, 0.0,
                                                 ALU.mult, ALU.max, moved_sq[:, n:n + 1]).then_inc(moved, 1)
                    dve.wait_ge(moved, 4)
                    dve.tensor_reduce(moved_max[:], moved_sq[:], AX.X, ALU.max).then_inc(moved, 1)
                    dve.wait_ge(moved, 5)
                    dve.tensor_scalar(settled[:], moved_max[:], STATE_TOL * STATE_TOL, None,
                                      ALU.is_le).then_inc(settled_ready, 1)
                    dve.wait_ge(settled_summed, 1)
                    dve.tensor_copy(settled_rows[:], settled_sum).then_inc(flag_ready, 1)
                    with unsettled(dve):
                        start(rest)
                        run(dve, rest, step, restart(lambda p: slice(0, 1)))

                @block.tensor
                def _(pe):
                    for k in range(HB):
                        pe.transpose(h_turn[k], h[:, k, :], ident[:]).then_inc(ends_turned, 1)

                    def turn(ph, p, k, first):
                        pe.wait_ge(ph.h_ready, first + 4 * p + k + 1)
                        pe.transpose(h_turn[k], h[:, k, :], ident[:]).then_inc(ph.h_turned, 1)

                    def step(ph, p, n, s, j):
                        first = 8 * n + 4 * j

                        def fill(b):
                            if b == 0:
                                pe.wait_ge(ph.xz_in[j], 16 * n + 16)
                            pe.wait_ge(ph.gates_ready, first + b + 5)
                            pe.matmul(z[:, b, :], ident[:], xz[:, j, b, :, :].rearrange("p g j -> p (g j)"),
                                      start=True, stop=False)

                        def add(k, b, parts):
                            if k == 0 and parts[:1] == [0] and b >= ph.by_pe:
                                pe.wait_ge(ph.pre_ready, ph.by_dve * (2 * n + j) + b - ph.by_pe + 1)
                            hi = wh_hi[:, k, :].rearrange("p (g b j) -> p b g j", g=4, b=HB)[:, b]
                            lo = wh_lo[:, k, :].rearrange("p (g b j) -> p b g j", g=4, b=HB)[:, b]
                            pairs = [(ht_hi, hi), (ht_hi, lo), (ht_lo, hi)] if ph.full else [(ht_hi, hi)]
                            for i in parts:
                                starts = k == 0 and i == 0 and b >= ph.by_pe
                                ends = k == HB - 1 and i == len(pairs) - 1
                                last = pe.matmul(z[:, b, :], pairs[i][0][:, k, :], pairs[i][1], start=starts, stop=ends)
                                if ends:
                                    last.then_inc(ph.summed, 1)

                        def hi_taken(k):
                            pe.wait_ge(ph.ht_hi_ready, first + 4 * p + k + 1)

                        def lo_taken(k):
                            if ph.full:
                                pe.wait_ge(ph.ht_lo_ready, first + 4 * p + k + 1)

                        every = [0, 1, 2] if ph.full else [0]
                        if ph.full:
                            hi_taken(0)
                            for b in range(HB):
                                add(0, b, [0, 1])
                                if b == 2:
                                    turn(ph, p, 1, first)
                            lo_taken(0)
                            for b in range(HB):
                                add(0, b, [2])
                            hi_taken(1)
                            lo_taken(1)
                            for b in range(HB - 1):
                                add(1, b, every)
                                if b < 2:
                                    turn(ph, p, 2 + b, first)
                        else:
                            fill(0)
                            fill(1)
                            turn(ph, p, 0, first)
                            turn(ph, p, 1, first)
                            hi_taken(0)
                            for b in range(HB):
                                add(0, b, every)
                            hi_taken(1)
                            for b in range(HB):
                                add(1, b, every)
                                if b < 2:
                                    turn(ph, p, 2 + b, first)
                        hi_taken(HB - 2 if ph.full else HB - 1)
                        lo_taken(HB - 2)
                        for b in range(HB):
                            add(2, b, every)
                            if ph.full and b == 0:
                                hi_taken(HB - 1)
                                lo_taken(HB - 1)
                            if ph.full and b == HB - 1:
                                turn(ph, p, 0, first + 4)
                            add(3, b, every)
                            if ph.full and b == 0:
                                add(1, HB - 1, every)

                    def begin(ph, p):
                        if ph.full:
                            turn(ph, p, 0, 4 * L * p)

                    def end(ph, p):
                        for k in range(1 if ph.full else 0, HB):
                            turn(ph, p, k, 4 * L * p + 4 * L)

                    run(pe, low, step, end, begin)
                    pe.wait_ge(wh_lo_ready, 2 * HB)
                    run(pe, full, step, end, begin)
                    pe.wait_ge(settled_ready, 1)
                    pe.matmul(settled_sum, settled[:], ones[:, 0:1], start=True, stop=True).then_inc(settled_summed, 1)
                    with unsettled(pe):
                        run(pe, rest, step, end, begin)


_INS = ['x', 'fside_BxS_0', 'cond_1024', 'L1_cond_Wx', 'L1_cond_Wh', 'L1_cond_b']
_OUTS = [((2, 2048, 512), 'float32')]


def kernel(**inputs):
    import numpy as _np
    import concourse.bacc as _bacc
    from concourse import mybir as _mybir
    from concourse.bass_utils import run_bass_kernel_spmd as _run

    nc = _bacc.Bacc("TRN2", target_bir_lowering=False, num_devices=1)
    arrays, args = {}, []
    for name in _INS:
        a = _np.ascontiguousarray(inputs[name])
        arrays[f"in_{name}_dram"] = a
        args.append(nc.dram_tensor(f"in_{name}_dram", a.shape, _mybir.dt.from_np(a.dtype), kind="ExternalInput").ap())
    for i, (shape, dtype) in enumerate(_OUTS):
        dt = _mybir.dt.from_np(_np.dtype(dtype))
        args.append(nc.dram_tensor(f"out_{i}_dram", shape, dt, kind="ExternalOutput").ap())
    sinkhorn_lstm(nc, *args)
    r = _run(nc, [arrays], core_ids=[0])
    return r.results[0]["out_0_dram"]
```
